# Optimizing a Trainium2 kernel written in Bass

```python
import numpy as np
import jax
import jax.numpy as jnp

def _softmax(x, axis=-1):
    return jax.nn.softmax(x, axis=axis)

def _gelu(x):
    return jax.nn.gelu(x, approximate=True)

def _silu(x):
    return jax.nn.silu(x)

def _sigmoid(x):
    return jax.nn.sigmoid(x)

def _layernorm(x, axis=-1, eps=1e-05):
    m = jnp.mean(x, axis=axis, keepdims=True)
    v = jnp.var(x, axis=axis, keepdims=True)
    return (x - m) / jnp.sqrt(v + eps)

def _scatter_add(tgt, idx, src, axis=0):
    return tgt.at[idx].add(src)

def _segment_sum(src, seg, n):
    return jax.ops.segment_sum(src, seg, n)
kernel_name = 'mk_seq_preln_d4_jaxref_r8_19bf1b'

def setup_inputs(seed: int=0):
    np.random.seed(seed)
    _w = jnp.asarray

    def _L0_attn_setup():
        import jax, jax.numpy as jnp
        import numpy as np
        H = 16
        GRID = 16
        TOK_PER_FRAME = GRID * GRID

        def _rope(x, pos, dim):
            half = dim // 2
            omega = jnp.arange(half, dtype=x.dtype) / (dim / 2.0)
            inv = 1.0 / 10000.0 ** omega
            freq = pos.astype(x.dtype)[:, None] * inv
            sin = jnp.concatenate([jnp.sin(freq), jnp.sin(freq)], axis=-1)
            cos = jnp.concatenate([jnp.cos(freq), jnp.cos(freq)], axis=-1)
            y = x.reshape(*x.shape[:-1], half, 2)
            y1, y2 = (y[..., 0], y[..., 1])
            rot = jnp.stack((-y2, y1), axis=-1).reshape(x.shape)
            return x * cos + rot * sin

        def _apply_3d_rope(qk, f_ids, h_ids, w_ids, d_dim):
            s = 0
            parts = []
            for pos in (f_ids, h_ids, w_ids):
                parts.append(_rope(qk[..., s:s + d_dim], pos, d_dim))
                s += d_dim
            if s < qk.shape[-1]:
                parts.append(qk[..., s:])
            return jnp.concatenate(parts, axis=-1)
        key = jax.random.key(seed)
        ks = jax.random.split(key, 5)
        D = 128
        B, N = (4, 256)
        sc = 0.02
        return {'hidden_states': jax.random.normal(ks[0], (B, N, D), jnp.float32), 'Wq': jax.random.normal(ks[1], (D, D), jnp.float32) * sc, 'bq': jnp.zeros((D,), jnp.float32), 'Wk': jax.random.normal(ks[2], (D, D), jnp.float32) * sc, 'bk': jnp.zeros((D,), jnp.float32), 'Wv': jax.random.normal(ks[3], (D, D), jnp.float32) * sc, 'bv': jnp.zeros((D,), jnp.float32), 'Wo': jax.random.normal(ks[4], (D, D), jnp.float32) * sc, 'bo': jnp.zeros((D,), jnp.float32)}
    _L0_attn_in = _L0_attn_setup()

    def _L0_ffn_setup():
        import jax, jax.numpy as jnp
        import numpy as np
        B, T, D = (4, 512, 128)
        E = 8
        TOP_K = 2
        FFN = 384
        HALF = FFN // 2

        def _kaiming_uniform(key, shape, fan_in):
            bound = 1.0 / np.sqrt(fan_in)
            return jax.random.uniform(key, shape, jnp.float32, -bound, bound)
        key = jax.random.key(seed)
        ks = jax.random.split(key, 7)
        x = jax.random.normal(ks[0], (B, T, D), jnp.float32)
        gate_w = _kaiming_uniform(ks[1], (E, D), D) * 0.01
        w_up = _kaiming_uniform(ks[2], (E, FFN, D), D)
        w_down = _kaiming_uniform(ks[3], (E, D, HALF), HALF)
        sg_gate = _kaiming_uniform(ks[4], (HALF, D), D)
        sg_up = _kaiming_uniform(ks[5], (HALF, D), D)
        sg_down = _kaiming_uniform(ks[6], (D, HALF), HALF)
        return {'x': x, 'gate_w': gate_w, 'w_up': w_up, 'w_down': w_down, 'sg_gate': sg_gate, 'sg_up': sg_up, 'sg_down': sg_down}
    _L0_ffn_in = _L0_ffn_setup()

    def _L1_attn_setup():
        import jax, jax.numpy as jnp
        import numpy as np
        HIDDEN = 128
        HEADS = 16
        BATCH = 2
        SEQ = 256
        key = jax.random.key(seed)
        k1, k2, k3 = jax.random.split(key, 3)
        x = jax.random.normal(k1, (BATCH, SEQ, HIDDEN), dtype=jnp.float32)
        w_qkv = jax.random.normal(k2, (3 * HIDDEN, HIDDEN), dtype=jnp.float32)
        w_o = jax.random.normal(k3, (HIDDEN, HIDDEN), dtype=jnp.float32)
        return {'x': x, 'w_qkv': w_qkv, 'w_o': w_o}
    _L1_attn_in = _L1_attn_setup()

    def _L1_ffn_setup():
        import math
        import jax, jax.numpy as jnp
        import numpy as np
        D_MODEL = 128
        D_FF = 512
        N_EXPERTS = 8
        CAPACITY_FACTOR = 1.25
        L, B = (64, 8)

        def _route(tokens, router_w):
            T = tokens.shape[0]
            E = router_w.shape[0]
            capacity = int(math.ceil(T / E * CAPACITY_FACTOR))
            logits = tokens @ router_w.T
            probs = jax.nn.softmax(logits, axis=-1)
            top1_idx = jnp.argmax(probs, axis=-1)
            top1_prob = jnp.max(probs, axis=-1)
            order = jnp.lexsort((-top1_prob, top1_idx))
            sorted_e = top1_idx[order]
            counts = jnp.bincount(top1_idx, length=E)
            start = jnp.cumsum(counts) - counts
            pos_in_group = jnp.arange(T) - start[sorted_e]
            keep_sorted = pos_in_group < capacity
            keep = jnp.zeros((T,), bool).at[order].set(keep_sorted)
            return jnp.where(keep, top1_idx, 0).astype(jnp.int32)
        key = jax.random.key(seed)
        ks = jax.random.split(key, 6)
        s_in = 1.0 / math.sqrt(D_MODEL)
        s_ff = 1.0 / math.sqrt(D_FF)
        return {'x': jax.random.normal(ks[0], (L, B, D_MODEL), dtype=jnp.float32), 'router_w': jax.random.uniform(ks[1], (N_EXPERTS, D_MODEL), minval=-s_in, maxval=s_in), 'W1': jax.random.uniform(ks[2], (N_EXPERTS, D_MODEL, D_FF), minval=-s_in, maxval=s_in), 'b1': jax.random.uniform(ks[3], (N_EXPERTS, D_FF), minval=-s_in, maxval=s_in), 'W2': jax.random.uniform(ks[4], (N_EXPERTS, D_FF, D_MODEL), minval=-s_ff, maxval=s_ff), 'b2': jax.random.uniform(ks[5], (N_EXPERTS, D_MODEL), minval=-s_ff, maxval=s_ff)}
    _L1_ffn_in = _L1_ffn_setup()

    def _L2_attn_setup():
        import jax, jax.numpy as jnp
        import numpy as np
        D_CONV = 4
        DT_RANK = 64
        D_STATE = 16

        def silu(v):
            return v * jax.nn.sigmoid(v)
        key = jax.random.key(seed)
        ks = jax.random.split(key, 10)
        B, L, d_model, d_inner = (2, 256, 128, 256)

        def nrm(k, shape, scale):
            return jax.random.normal(k, shape, dtype=jnp.float32) * scale
        A = jnp.tile(jnp.arange(1, D_STATE + 1, dtype=jnp.float32), (d_inner, 1))
        return {'x': nrm(ks[0], (B, L, d_model), 1.0), 'W_in': nrm(ks[1], (d_model, 2 * d_inner), d_model ** (-0.5)), 'conv_w': nrm(ks[2], (d_inner, D_CONV), D_CONV ** (-0.5)), 'conv_b': nrm(ks[3], (d_inner,), 0.02), 'W_x': nrm(ks[4], (d_inner, DT_RANK + 2 * D_STATE), d_inner ** (-0.5)), 'W_dt': nrm(ks[5], (DT_RANK, d_inner), DT_RANK ** (-0.5)), 'b_dt': nrm(ks[6], (d_inner,), 0.02), 'A_log': jnp.log(A), 'D': jnp.ones((d_inner,), dtype=jnp.float32), 'W_out': nrm(ks[7], (d_inner, d_model), d_inner ** (-0.5))}
    _L2_attn_in = _L2_attn_setup()

    def _L2_ffn_setup():
        import jax, jax.numpy as jnp
        import numpy as np
        B, S, D = (2, 128, 128)
        H = 64
        E = 16
        K = 2
        HS = 2 * H
        ROUTE_SCALE = 1.0

        def _gated_mlp_act(y):
            u, g = jnp.split(y, 2, axis=-1)
            return u * jax.nn.silu(g)
        key = jax.random.key(seed)
        ks = jax.random.split(key, 6)
        s = 0.02
        return {'x': jax.random.normal(ks[0], (B, S, D), dtype=jnp.float32), 'Wg': jax.random.normal(ks[1], (E, D), dtype=jnp.float32) * s, 'W1': jax.random.normal(ks[2], (E, D, 2 * H), dtype=jnp.float32) * s, 'W2': jax.random.normal(ks[3], (E, H, D), dtype=jnp.float32) * s, 'Ws1': jax.random.normal(ks[4], (D, 2 * HS), dtype=jnp.float32) * s, 'Ws2': jax.random.normal(ks[5], (HS, D), dtype=jnp.float32) * s}
    _L2_ffn_in = _L2_ffn_setup()

    def _L3_attn_setup():
        import jax, jax.numpy as jnp
        import numpy as np
        B_, L_, DM, E, H, R, K = (4, 512, 128, 256, 128, 64, 4)
        NUM_BLOCKS = 4

        def _forward(x, Win, conv_w, conv_b, Wx, Wdt, bdt, A_log, D, ln_g, ln_b, Wout, res_scale):
            b, l, _ = x.shape
            proj = x @ Win
            xp, z, Bp = jnp.split(proj, 3, axis=-1)
            xpad = jnp.pad(xp, ((0, 0), (K - 1, 0), (0, 0)))
            xc = sum((xpad[:, k:k + l, :] * conv_w[:, k] for k in range(K))) + conv_b
            xs = jax.nn.silu(xc)
            x_dbl = xs @ Wx
            dr, C = (x_dbl[..., :R], x_dbl[..., R:])
            delta = jax.nn.softplus(dr @ Wdt + bdt)
            Bm = jax.nn.softplus(Bp)
            A = -jnp.exp(A_log)
            dlt = jnp.clip(delta, 1e-06, 100.0)
            a_seq = jnp.exp(dlt[:, :, 0:1] * A[0])
            bd_seq = (dlt[:, :, 0] * Bm[:, :, 0] * xs[:, :, 0])[..., None]

            def step(s, inp):
                a_t, bd_t, c_t = inp
                s = a_t * s + bd_t
                return (s, jnp.sum(c_t * s, axis=-1))
            s0 = jnp.zeros((b, H), x.dtype)
            _, y_sc = jax.lax.scan(step, s0, (a_seq.transpose(1, 0, 2), bd_seq.transpose(1, 0, 2), C.transpose(1, 0, 2)))
            y = y_sc.transpose(1, 0)[..., None] + D * xs
            mu = jnp.mean(y, axis=-1, keepdims=True)
            var = jnp.var(y, axis=-1, keepdims=True)
            yn = (y - mu) / jnp.sqrt(var + 1e-05) * ln_g + ln_b
            yg = yn * jax.nn.sigmoid(z)
            return yg @ Wout * res_scale
        key = jax.random.key(seed)
        ks = jax.random.split(key, 7)
        x = jax.random.normal(ks[0], (B_, L_, DM), jnp.float32)
        Win = jax.random.normal(ks[1], (DM, 3 * E), jnp.float32) * 0.02
        conv_w = jax.random.normal(ks[2], (E, K), jnp.float32) * 0.2
        conv_b = jnp.zeros((E,), jnp.float32)
        Wx = jax.random.normal(ks[3], (E, R + H), jnp.float32) * 0.02
        Wdt = jax.random.normal(ks[4], (R, E), jnp.float32) * 0.1
        bdt = jnp.zeros((E,), jnp.float32)
        block = jnp.arange(1, H // NUM_BLOCKS + 1, dtype=jnp.float32)
        A_log = jnp.broadcast_to(jnp.log(jnp.tile(block, NUM_BLOCKS))[None, :], (E, H)) + 0.0
        D = jnp.ones((E,), jnp.float32)
        ln_g = jnp.ones((E,), jnp.float32)
        ln_b = jnp.zeros((E,), jnp.float32)
        Wout = jax.random.normal(ks[5], (E, DM), jnp.float32) * 0.02
        res_scale = jnp.ones((1,), jnp.float32)
        return dict(x=x, Win=Win, conv_w=conv_w, conv_b=conv_b, Wx=Wx, Wdt=Wdt, bdt=bdt, A_log=A_log, D=D, ln_g=ln_g, ln_b=ln_b, Wout=Wout, res_scale=res_scale)
    _L3_attn_in = _L3_attn_setup()

    def _L3_ffn_setup():
        import jax, jax.numpy as jnp
        import numpy as np
        import math
        BETA = 0.9
        THRESHOLD = 1.0
        NUM_STEPS = 5
        ALPHA = 2.0

        @jax.custom_vjp
        def spike_fn(u):
            return (u > 0).astype(u.dtype)

        def _spike_fwd(u):
            return (spike_fn(u), u)

        def _spike_bwd(u, g):
            s = jnp.pi / 2.0 * ALPHA * u
            return (g * (ALPHA / 2.0) / (1.0 + s * s),)
        spike_fn.defvjp(_spike_fwd, _spike_bwd)
        key = jax.random.key(seed)
        k1, k2, k3 = jax.random.split(key, 3)
        n_embd = 128
        x = jax.random.normal(k1, (4, 256, n_embd), dtype=jnp.float32)
        W_fc = jax.random.normal(k2, (4 * n_embd, n_embd), dtype=jnp.float32) / math.sqrt(n_embd)
        W_proj = jax.random.normal(k3, (n_embd, 4 * n_embd), dtype=jnp.float32) / math.sqrt(4 * n_embd)
        return {'x': x, 'W_fc': W_fc, 'W_proj': W_proj}
    _L3_ffn_in = _L3_ffn_setup()
    _d = {'L0_attn_hidden_states': _L0_attn_in['hidden_states'], 'L0_attn_Wq': _L0_attn_in['Wq'], 'L0_attn_bq': _L0_attn_in['bq'], 'L0_attn_Wk': _L0_attn_in['Wk'], 'L0_attn_bk': _L0_attn_in['bk'], 'L0_attn_Wv': _L0_attn_in['Wv'], 'L0_attn_bv': _L0_attn_in['bv'], 'L0_attn_Wo': _L0_attn_in['Wo'], 'L0_attn_bo': _L0_attn_in['bo'], 'L0_ffn_gate_w': _L0_ffn_in['gate_w'], 'L0_ffn_w_up': _L0_ffn_in['w_up'], 'L0_ffn_w_down': _L0_ffn_in['w_down'], 'L0_ffn_sg_gate': _L0_ffn_in['sg_gate'], 'L0_ffn_sg_up': _L0_ffn_in['sg_up'], 'L0_ffn_sg_down': _L0_ffn_in['sg_down'], 'L1_attn_w_qkv': _L1_attn_in['w_qkv'], 'L1_attn_w_o': _L1_attn_in['w_o'], 'L1_ffn_router_w': _L1_ffn_in['router_w'], 'L1_ffn_W1': _L1_ffn_in['W1'], 'L1_ffn_b1': _L1_ffn_in['b1'], 'L1_ffn_W2': _L1_ffn_in['W2'], 'L1_ffn_b2': _L1_ffn_in['b2'], 'L2_attn_W_in': _L2_attn_in['W_in'], 'L2_attn_conv_w': _L2_attn_in['conv_w'], 'L2_attn_conv_b': _L2_attn_in['conv_b'], 'L2_attn_W_x': _L2_attn_in['W_x'], 'L2_attn_W_dt': _L2_attn_in['W_dt'], 'L2_attn_b_dt': _L2_attn_in['b_dt'], 'L2_attn_A_log': _L2_attn_in['A_log'], 'L2_attn_D': _L2_attn_in['D'], 'L2_attn_W_out': _L2_attn_in['W_out'], 'L2_ffn_Wg': _L2_ffn_in['Wg'], 'L2_ffn_W1': _L2_ffn_in['W1'], 'L2_ffn_W2': _L2_ffn_in['W2'], 'L2_ffn_Ws1': _L2_ffn_in['Ws1'], 'L2_ffn_Ws2': _L2_ffn_in['Ws2'], 'L3_attn_Win': _L3_attn_in['Win'], 'L3_attn_conv_w': _L3_attn_in['conv_w'], 'L3_attn_conv_b': _L3_attn_in['conv_b'], 'L3_attn_Wx': _L3_attn_in['Wx'], 'L3_attn_Wdt': _L3_attn_in['Wdt'], 'L3_attn_bdt': _L3_attn_in['bdt'], 'L3_attn_A_log': _L3_attn_in['A_log'], 'L3_attn_D': _L3_attn_in['D'], 'L3_attn_ln_g': _L3_attn_in['ln_g'], 'L3_attn_ln_b': _L3_attn_in['ln_b'], 'L3_attn_Wout': _L3_attn_in['Wout'], 'L3_attn_res_scale': _L3_attn_in['res_scale'], 'L3_ffn_W_fc': _L3_ffn_in['W_fc'], 'L3_ffn_W_proj': _L3_ffn_in['W_proj']}
    _x0 = _d['L0_attn_hidden_states']
    _d['L0_attn_hidden_states'] = jax.random.normal(jax.random.fold_in(jax.random.key(seed), 1), (4, 1024, 128), dtype=_x0.dtype)
    del _x0
    return _d

def reference(L0_attn_hidden_states, L0_attn_Wq, L0_attn_bq, L0_attn_Wk, L0_attn_bk, L0_attn_Wv, L0_attn_bv, L0_attn_Wo, L0_attn_bo, L0_ffn_gate_w, L0_ffn_w_up, L0_ffn_w_down, L0_ffn_sg_gate, L0_ffn_sg_up, L0_ffn_sg_down, L1_attn_w_qkv, L1_attn_w_o, L1_ffn_router_w, L1_ffn_W1, L1_ffn_b1, L1_ffn_W2, L1_ffn_b2, L2_attn_W_in, L2_attn_conv_w, L2_attn_conv_b, L2_attn_W_x, L2_attn_W_dt, L2_attn_b_dt, L2_attn_A_log, L2_attn_D, L2_attn_W_out, L2_ffn_Wg, L2_ffn_W1, L2_ffn_W2, L2_ffn_Ws1, L2_ffn_Ws2, L3_attn_Win, L3_attn_conv_w, L3_attn_conv_b, L3_attn_Wx, L3_attn_Wdt, L3_attn_bdt, L3_attn_A_log, L3_attn_D, L3_attn_ln_g, L3_attn_ln_b, L3_attn_Wout, L3_attn_res_scale, L3_ffn_W_fc, L3_ffn_W_proj):

    def _L0_attn_ref(hidden_states, Wq, bq, Wk, bk, Wv, bv, Wo, bo):
        import jax, jax.numpy as jnp
        import numpy as np
        H = 16
        GRID = 16
        TOK_PER_FRAME = GRID * GRID

        def _rope(x, pos, dim):
            half = dim // 2
            omega = jnp.arange(half, dtype=x.dtype) / (dim / 2.0)
            inv = 1.0 / 10000.0 ** omega
            freq = pos.astype(x.dtype)[:, None] * inv
            sin = jnp.concatenate([jnp.sin(freq), jnp.sin(freq)], axis=-1)
            cos = jnp.concatenate([jnp.cos(freq), jnp.cos(freq)], axis=-1)
            y = x.reshape(*x.shape[:-1], half, 2)
            y1, y2 = (y[..., 0], y[..., 1])
            rot = jnp.stack((-y2, y1), axis=-1).reshape(x.shape)
            return x * cos + rot * sin

        def _apply_3d_rope(qk, f_ids, h_ids, w_ids, d_dim):
            s = 0
            parts = []
            for pos in (f_ids, h_ids, w_ids):
                parts.append(_rope(qk[..., s:s + d_dim], pos, d_dim))
                s += d_dim
            if s < qk.shape[-1]:
                parts.append(qk[..., s:])
            return jnp.concatenate(parts, axis=-1)
        B, N, D = hidden_states.shape
        hd = D // H
        d_dim = 2 * (hd // 3 // 2)

        def heads(x):
            return x.reshape(B, N, H, hd).transpose(0, 2, 1, 3)
        q = heads(hidden_states @ Wq + bq)
        k = heads(hidden_states @ Wk + bk)
        v = heads(hidden_states @ Wv + bv)
        ids = jnp.arange(N)
        f_ids = ids // TOK_PER_FRAME
        rem = ids - TOK_PER_FRAME * f_ids
        h_ids = rem // GRID
        w_ids = rem - GRID * h_ids
        q = _apply_3d_rope(q, f_ids, h_ids, w_ids, d_dim)
        k = _apply_3d_rope(k, f_ids, h_ids, w_ids, d_dim)
        scale = hd ** (-0.5)
        attn = jnp.einsum('bhqd,bhkd->bhqk', q, k) * scale
        attn = jax.nn.softmax(attn.astype(jnp.float32), axis=-1).astype(q.dtype)
        ctx = jnp.einsum('bhqk,bhkd->bhqd', attn, v)
        ctx = ctx.transpose(0, 2, 1, 3).reshape(B, N, D)
        return ctx @ Wo + bo

    def _L0_ffn_ref(x, gate_w, w_up, w_down, sg_gate, sg_up, sg_down):
        import jax, jax.numpy as jnp
        import numpy as np
        B, T, D = (4, 512, 128)
        E = 8
        TOP_K = 2
        FFN = 384
        HALF = FFN // 2

        def _kaiming_uniform(key, shape, fan_in):
            bound = 1.0 / np.sqrt(fan_in)
            return jax.random.uniform(key, shape, jnp.float32, -bound, bound)
        b, t, d = x.shape
        xf = x.reshape(b * t, d)
        N = xf.shape[0]
        logits = xf @ gate_w.T
        topk_logits, topk_idx = jax.lax.top_k(logits, TOP_K)
        topk_w = jax.nn.softmax(topk_logits.astype(jnp.float32), axis=-1).astype(x.dtype)
        comb = jnp.zeros((N, E), x.dtype).at[jnp.arange(N)[:, None], topk_idx].add(topk_w)
        wg = w_up[:, :HALF, :]
        wu = w_up[:, HALF:, :]
        out = jnp.zeros_like(xf)
        for e in range(E):
            g = xf @ wg[e].T
            u = xf @ wu[e].T
            y = jax.nn.silu(g) * u @ w_down[e].T
            out = out + comb[:, e:e + 1] * y
        shared = jax.nn.silu(xf @ sg_gate.T) * (xf @ sg_up.T) @ sg_down.T
        return (shared + out).reshape(b, t, d)

    def _L1_attn_ref(x, w_qkv, w_o):
        import jax, jax.numpy as jnp
        import numpy as np
        HIDDEN = 128
        HEADS = 16
        BATCH = 2
        SEQ = 256
        b, s, hid = x.shape
        heads = HEADS
        d = hid // heads
        qkv = x @ w_qkv.T * hid ** (-0.5)
        qkv = qkv.reshape(b, s, 3, heads, d)
        q = jnp.transpose(qkv[:, :, 0], (0, 2, 1, 3))
        k = jnp.transpose(qkv[:, :, 1], (0, 2, 1, 3))
        v = jnp.transpose(qkv[:, :, 2], (0, 2, 1, 3))
        scores = jnp.einsum('bhqd,bhkd->bhqk', q, k) * d ** (-0.5)
        attn = jax.nn.softmax(scores, axis=-1) * (s / np.sqrt(s - 1.0))
        out = jnp.einsum('bhqk,bhkd->bhqd', attn, v) * s ** (-0.5)
        out = jnp.transpose(out, (0, 2, 1, 3)).reshape(b, s, hid)
        return out @ w_o.T * hid ** (-0.5)

    def _L1_ffn_ref(x, router_w, W1, b1, W2, b2):
        import math
        import jax, jax.numpy as jnp
        import numpy as np
        D_MODEL = 128
        D_FF = 512
        N_EXPERTS = 8
        CAPACITY_FACTOR = 1.25
        L, B = (64, 8)

        def _route(tokens, router_w):
            T = tokens.shape[0]
            E = router_w.shape[0]
            capacity = int(math.ceil(T / E * CAPACITY_FACTOR))
            logits = tokens @ router_w.T
            probs = jax.nn.softmax(logits, axis=-1)
            top1_idx = jnp.argmax(probs, axis=-1)
            top1_prob = jnp.max(probs, axis=-1)
            order = jnp.lexsort((-top1_prob, top1_idx))
            sorted_e = top1_idx[order]
            counts = jnp.bincount(top1_idx, length=E)
            start = jnp.cumsum(counts) - counts
            pos_in_group = jnp.arange(T) - start[sorted_e]
            keep_sorted = pos_in_group < capacity
            keep = jnp.zeros((T,), bool).at[order].set(keep_sorted)
            return jnp.where(keep, top1_idx, 0).astype(jnp.int32)
        Lx, Bx, D = x.shape
        T = Lx * Bx
        E = router_w.shape[0]
        tokens = x.reshape(T, D)
        final_e = _route(tokens, router_w)
        out = jnp.zeros_like(tokens)
        for e in range(E):
            h = jax.nn.relu(tokens @ W1[e] + b1[e])
            y = h @ W2[e] + b2[e]
            out = out + jnp.where((final_e == e)[:, None], y, 0.0)
        return out.reshape(Lx, Bx, D)

    def _L2_attn_ref(x, W_in, conv_w, conv_b, W_x, W_dt, b_dt, A_log, D, W_out):
        import jax, jax.numpy as jnp
        import numpy as np
        D_CONV = 4
        DT_RANK = 64
        D_STATE = 16

        def silu(v):
            return v * jax.nn.sigmoid(v)
        B, L, _ = x.shape
        d_inner = W_dt.shape[1]
        xz = x @ W_in
        xb, z = jnp.split(xz, 2, axis=-1)
        xp = jnp.pad(xb, ((0, 0), (D_CONV - 1, 0), (0, 0)))
        xc = sum((xp[:, k:k + L, :] * conv_w[:, k] for k in range(D_CONV))) + conv_b
        xb = silu(xc)
        x_dbl = xb @ W_x
        dt_low, Bm, Cm = jnp.split(x_dbl, [DT_RANK, DT_RANK + D_STATE], axis=-1)
        dt = jax.nn.softplus(dt_low @ W_dt + b_dt)
        A = -jnp.exp(A_log)

        def step(h, inp):
            dt_t, B_t, C_t, x_t = inp
            dA = jnp.exp(A * dt_t[..., None])
            h = h * dA + (x_t * dt_t)[..., None] * B_t[:, None, :]
            y = jnp.einsum('bdn,bn->bd', h, C_t)
            return (h, y)
        xs = (dt.swapaxes(0, 1), Bm.swapaxes(0, 1), Cm.swapaxes(0, 1), xb.swapaxes(0, 1))
        h0 = jnp.zeros((B, d_inner, D_STATE), dtype=x.dtype)
        _, ys = jax.lax.scan(step, h0, xs)
        y = ys.swapaxes(0, 1) + xb * D
        out = y * silu(z)
        return out @ W_out

    def _L2_ffn_ref(x, Wg, W1, W2, Ws1, Ws2):
        import jax, jax.numpy as jnp
        import numpy as np
        B, S, D = (2, 128, 128)
        H = 64
        E = 16
        K = 2
        HS = 2 * H
        ROUTE_SCALE = 1.0

        def _gated_mlp_act(y):
            u, g = jnp.split(y, 2, axis=-1)
            return u * jax.nn.silu(g)
        x_shape = x.shape
        xf = x.reshape(-1, D)
        scores = jax.nn.softmax(xf @ Wg.T, axis=-1)
        wk, idx = jax.lax.top_k(scores, K)
        wk = wk * ROUTE_SCALE
        cw = jnp.sum(jax.nn.one_hot(idx, E, dtype=xf.dtype) * wk[..., None], axis=1)
        h = _gated_mlp_act(jnp.einsum('td,edh->teh', xf, W1))
        z = jnp.einsum('te,teh,ehd->td', cw, h, W2)
        ys = _gated_mlp_act(xf @ Ws1) @ Ws2
        return (z + ys).reshape(x_shape)

    def _L3_attn_ref(x, Win, conv_w, conv_b, Wx, Wdt, bdt, A_log, D, ln_g, ln_b, Wout, res_scale):
        import jax, jax.numpy as jnp
        import numpy as np
        B_, L_, DM, E, H, R, K = (4, 512, 128, 256, 128, 64, 4)
        NUM_BLOCKS = 4

        def _forward(x, Win, conv_w, conv_b, Wx, Wdt, bdt, A_log, D, ln_g, ln_b, Wout, res_scale):
            b, l, _ = x.shape
            proj = x @ Win
            xp, z, Bp = jnp.split(proj, 3, axis=-1)
            xpad = jnp.pad(xp, ((0, 0), (K - 1, 0), (0, 0)))
            xc = sum((xpad[:, k:k + l, :] * conv_w[:, k] for k in range(K))) + conv_b
            xs = jax.nn.silu(xc)
            x_dbl = xs @ Wx
            dr, C = (x_dbl[..., :R], x_dbl[..., R:])
            delta = jax.nn.softplus(dr @ Wdt + bdt)
            Bm = jax.nn.softplus(Bp)
            A = -jnp.exp(A_log)
            dlt = jnp.clip(delta, 1e-06, 100.0)
            a_seq = jnp.exp(dlt[:, :, 0:1] * A[0])
            bd_seq = (dlt[:, :, 0] * Bm[:, :, 0] * xs[:, :, 0])[..., None]

            def step(s, inp):
                a_t, bd_t, c_t = inp
                s = a_t * s + bd_t
                return (s, jnp.sum(c_t * s, axis=-1))
            s0 = jnp.zeros((b, H), x.dtype)
            _, y_sc = jax.lax.scan(step, s0, (a_seq.transpose(1, 0, 2), bd_seq.transpose(1, 0, 2), C.transpose(1, 0, 2)))
            y = y_sc.transpose(1, 0)[..., None] + D * xs
            mu = jnp.mean(y, axis=-1, keepdims=True)
            var = jnp.var(y, axis=-1, keepdims=True)
            yn = (y - mu) / jnp.sqrt(var + 1e-05) * ln_g + ln_b
            yg = yn * jax.nn.sigmoid(z)
            return yg @ Wout * res_scale
        return _forward(x, Win, conv_w, conv_b, Wx, Wdt, bdt, A_log, D, ln_g, ln_b, Wout, res_scale)

    def _L3_ffn_ref(x, W_fc, W_proj):
        import jax, jax.numpy as jnp
        import numpy as np
        import math
        BETA = 0.9
        THRESHOLD = 1.0
        NUM_STEPS = 5
        ALPHA = 2.0

        @jax.custom_vjp
        def spike_fn(u):
            return (u > 0).astype(u.dtype)

        def _spike_fwd(u):
            return (spike_fn(u), u)

        def _spike_bwd(u, g):
            s = jnp.pi / 2.0 * ALPHA * u
            return (g * (ALPHA / 2.0) / (1.0 + s * s),)
        spike_fn.defvjp(_spike_fwd, _spike_bwd)
        h = jnp.square(jax.nn.relu(jnp.einsum('bsd,fd->bsf', x, W_fc)))
        y = jnp.einsum('bsf,df->bsd', h, W_proj)

        def step(mem, _):
            reset = jax.lax.stop_gradient(spike_fn(mem - THRESHOLD))
            mem_new = BETA * mem + y - reset * THRESHOLD
            spk = spike_fn(mem_new - THRESHOLD)
            return (mem_new, spk)
        mem0 = jnp.zeros_like(y)
        _, spks = jax.lax.scan(step, mem0, None, length=NUM_STEPS)
        return jnp.sum(spks, axis=0) / NUM_STEPS
    x = L0_attn_hidden_states
    x = x + _L0_attn_ref(_layernorm(x, axis=-1), L0_attn_Wq, L0_attn_bq, L0_attn_Wk, L0_attn_bk, L0_attn_Wv, L0_attn_bv, L0_attn_Wo, L0_attn_bo)
    x = x + _L0_ffn_ref(_layernorm(x, axis=-1), L0_ffn_gate_w, L0_ffn_w_up, L0_ffn_w_down, L0_ffn_sg_gate, L0_ffn_sg_up, L0_ffn_sg_down)
    x = x + _L1_attn_ref(_layernorm(x, axis=-1), L1_attn_w_qkv, L1_attn_w_o)
    x = x + _L1_ffn_ref(_layernorm(x, axis=-1), L1_ffn_router_w, L1_ffn_W1, L1_ffn_b1, L1_ffn_W2, L1_ffn_b2)
    x = x + _L2_attn_ref(_layernorm(x, axis=-1), L2_attn_W_in, L2_attn_conv_w, L2_attn_conv_b, L2_attn_W_x, L2_attn_W_dt, L2_attn_b_dt, L2_attn_A_log, L2_attn_D, L2_attn_W_out)
    x = x + _L2_ffn_ref(_layernorm(x, axis=-1), L2_ffn_Wg, L2_ffn_W1, L2_ffn_W2, L2_ffn_Ws1, L2_ffn_Ws2)
    x = x + _L3_attn_ref(_layernorm(x, axis=-1), L3_attn_Win, L3_attn_conv_w, L3_attn_conv_b, L3_attn_Wx, L3_attn_Wdt, L3_attn_bdt, L3_attn_A_log, L3_attn_D, L3_attn_ln_g, L3_attn_ln_b, L3_attn_Wout, L3_attn_res_scale)
    x = x + _L3_ffn_ref(_layernorm(x, axis=-1), L3_ffn_W_fc, L3_ffn_W_proj)
    return x

_drawn_inputs = setup_inputs


def setup_inputs(seed=0):
    import zlib

    import numpy as np

    out = dict(_drawn_inputs(seed))
    spreads = {'L0_attn_bq': (0.0, 0.8),
     'L0_attn_bk': (0.0, 0.8),
     'L0_attn_bv': (0.0, 0.1),
     'L0_attn_bo': (0.0, 0.1),
     'L2_attn_D': (1.0, 0.2),
     'L3_attn_conv_b': (0.0, 0.1),
     'L3_attn_bdt': (0.0, 2.0),
     'L3_attn_D': (1.0, 0.6),
     'L3_attn_ln_g': (1.0, 0.6),
     'L3_attn_ln_b': (0.0, 0.347)}
    factors = {'L0_attn_Wq': 8.0,
     'L0_attn_Wk': 8.0,
     'L0_attn_Wv': 3.457,
     'L2_attn_b_dt': 5.508,
     'L2_ffn_Wg': 8.0,
     'L2_ffn_W1': 8.0,
     'L2_ffn_W2': 8.0,
     'L2_ffn_Ws1': 5.337,
     'L2_ffn_Ws2': 5.419,
     'L3_attn_Wx': 64.0,
     'L3_attn_Wdt': 64.0,
     'L3_attn_A_log': 64.0}
    for name, (base, spread) in spreads.items():
        noise = np.random.default_rng([zlib.crc32(name.encode()), seed]).standard_normal(out[name].shape)
        drawn = base * np.exp(spread * noise) if base else spread * noise
        out[name] = jnp.asarray(drawn.astype(out[name].dtype))
    for name, factor in factors.items():
        out[name] = (out[name] * factor).astype(out[name].dtype)
    return out
```

```python
from contextlib import ExitStack

import numpy as np

import concourse.bass as bass
from concourse import mybir
from concourse.alu_op_type import AluOpType as ALU

ACT = mybir.ActivationFunctionType
F32 = mybir.dt.float32
BF16 = mybir.dt.bfloat16
AX = mybir.AxisListType

P = 128
BATCH, SEQ = 4, 1024
TOK = BATCH * SEQ
CH = 512
NCH = TOK // CH
NT = TOK // P
HEADS, HD = 16, 8
PAIRS = HEADS // 2
NPAIR = BATCH * PAIRS
EPS = 1e-5

SPECIAL = 32
STACK = 50
Q_PARTS = [(0, 0), (8, 0), (16, 1), (24, 1), (34, 0), (42, 2)]
K_PARTS = [(0, 0), (8, 1), (16, 0), (24, 1), (34, 2), (42, 0)]


class Stage:

    def __init__(self, nc, name):
        self.nc, self.name, self.ctx, self.sems = nc, name, ExitStack(), []

    def __enter__(self):
        return self

    def __exit__(self, *a):
        for sem in self.sems:
            self.nc.sync.sem_clear(sem)
        self.ctx.close()

    def sb(self, name, shape, dt=F32):
        return self.ctx.enter_context(self.nc.sbuf_tensor(f"{self.name}_{name}", shape, dt))

    def ps(self, name, shape, dt=F32):
        return self.ctx.enter_context(self.nc.psum_tensor(f"{self.name}_{name}", shape, dt))

    def sem(self, name):
        self.sems.append(self.ctx.enter_context(self.nc.semaphore(f"{self.name}_{name}")))
        return self.sems[-1]


def chunk(c):
    return bass.ds(c * CH, CH)


def load_stage(nc, g, x, ident):
    with Stage(nc, "load") as s:
        xin = s.sb("xin", [P, NT, P])
        ps = s.ps("ps", [P, NCH, CH])
        const_in, x_in = s.sem("const_in"), [s.sem(f"x_in{i}") for i in range(4)]
        turned, copied = s.sem("turned"), s.sem("copied")
        ready = s.sem("ready")
        src = x.rearrange("b (t p) d -> p (b t) d", p=P)
        q = NT // 4
        with nc.Block() as block:
            @block.sync
            def _(sp):
                sp.dma_start(g.ident[:, :], ident).then_inc(const_in, 16)
                for i in range(4):
                    sp.dma_start(xin[:, i * q:(i + 1) * q, :], src[:, i * q:(i + 1) * q, :]).then_inc(x_in[i], 16)

            @block.gpsimd
            def _(pool):
                pool.memset(g.eps[:, :], EPS).then_inc(ready, 1)
                pool.memset(g.ones[:, :], 1.0).then_inc(ready, 1)
                pool.wait_ge(const_in, 16)
                pool.tensor_copy(g.ident_b[:, :], g.ident[:, :]).then_inc(ready, 1)
                pool.wait_ge(ready, 3)

            @block.tensor
            def _(pe):
                pe.wait_ge(const_in, 16)
                for t in range(NT):
                    if t % q == 0:
                        pe.wait_ge(x_in[t // q], 16)
                    mm = pe.transpose(ps[:, t // 4, (t % 4) * P:(t % 4 + 1) * P], xin[:, t, :], g.ident[:, :])
                    if t % 4 == 3:
                        mm.then_inc(turned, 1)

            @block.vector
            def _(dve):
                for c in range(NCH):
                    dve.wait_ge(turned, c + 1)
                    dve.tensor_copy(g.xT[:, c * CH:(c + 1) * CH], ps[:, c, :]).then_inc(copied, 1)
                dve.wait_ge(copied, NCH)


def norm_stage(nc, g, name, src=None, dst=None):
    src, dst = src or [g.xT[:, :]], dst or [g.xn[:, :]]
    k = len(src)
    with Stage(nc, name) as s:
        sq = s.sb("sq", [P, k, TOK])
        mean_w = s.sb("mean_w", [P, P])
        std, rstd = s.sb("std", [P, NT]), s.sb("rstd", [P, NT])
        mean_ps = s.ps("mean", [P, 3, CH])
        var_ps = s.ps("var", [P, NT])
        rs_ps = s.ps("rs", [P, 4, CH])
        w_ready, mean_ready, centred, squared = (s.sem(x) for x in ("w_ready", "mean_ready", "centred", "squared"))
        var_ready, std_ready, rstd_ready = s.sem("var_ready"), s.sem("std_ready"), s.sem("rstd_ready")
        rows_ready, scaled = s.sem("rows_ready"), s.sem("scaled")
        cols = lambda c: slice(c * CH, (c + 1) * CH)
        with nc.Block() as block:
            @block.gpsimd
            def _(pool):
                pool.memset(mean_w[:, :], 1.0 / (k * P)).then_inc(w_ready, 1)

            @block.tensor
            def _(pe):
                pe.wait_ge(w_ready, 1)
                for c in range(NCH):
                    if c >= 3:
                        pe.wait_ge(centred, k * (c - 2))
                    for i in range(k):
                        mm = pe.matmul(mean_ps[:, c % 3, :], mean_w[:, :], src[i][:, cols(c)],
                                       start=i == 0, stop=i == k - 1)
                    mm.then_inc(mean_ready, 1)
                for t in range(NT):
                    if t % 4 == 0:
                        pe.wait_ge(squared, k * (t // 4 + 1))
                    for i in range(k):
                        mm = pe.matmul(var_ps[:, t:t + 1], sq[:, i, t * P:(t + 1) * P], mean_w[:, 0:1],
                                       start=i == 0, stop=i == k - 1)
                mm.then_inc(var_ready, 1)
                pe.wait_ge(rstd_ready, 1)
                for t in range(NT):
                    if t % 4 == 0 and t >= 16:
                        pe.wait_ge(scaled, k * (t // 4 - 3))
                    mm = pe.matmul(rs_ps[:, (t // 4) % 4, (t % 4) * P:(t % 4 + 1) * P],
                                   rstd[:, t:t + 1].to_broadcast([P, P]), g.ident[:, :], start=True, stop=True)
                    if t % 4 == 3:
                        mm.then_inc(rows_ready, 1)

            @block.vector
            def _(dve):
                for c in range(NCH):
                    dve.wait_ge(mean_ready, c + 1)
                    for i in range(k):
                        dve.tensor_tensor(dst[i][:, cols(c)], src[i][:, cols(c)], mean_ps[:, c % 3, :],
                                          ALU.subtract).then_inc(centred, 1)
                dve.wait_ge(std_ready, 1)
                dve.reciprocal(rstd[:, :], std[:, :]).then_inc(rstd_ready, 1)
                for c in range(NCH):
                    dve.wait_ge(rows_ready, c + 1)
                    for i in range(k):
                        dve.tensor_tensor(dst[i][:, cols(c)], dst[i][:, cols(c)], rs_ps[:, c % 4, :],
                                          ALU.mult).then_inc(scaled, 1)
                dve.wait_ge(scaled, k * NCH)

            @block.scalar
            def _(act):
                for c in range(NCH):
                    for i in range(k):
                        act.wait_ge(centred, k * c + i + 1)
                        act.activation(sq[:, i, cols(c)], dst[i][:, cols(c)], ACT.Square).then_inc(squared, 1)
                act.wait_ge(var_ready, 1)
                act.activation(std[:, :], var_ps[:, :], ACT.Sqrt, bias=g.eps[:, :]).then_inc(std_ready, 1)


def store_stage(nc, g, out):
    with Stage(nc, "store") as s:
        y = s.sb("y", [P, NT, P])
        ps = s.ps("ps", [P, NCH, CH])
        turned, copied, stored = s.sem("turned"), s.sem("copied"), s.sem("stored")
        dst = out.rearrange("b (t p) d -> p (b t) d", p=P)
        with nc.Block() as block:
            @block.tensor
            def _(pe):
                for t in range(NT):
                    mm = pe.transpose(ps[:, t // 4, (t % 4) * P:(t % 4 + 1) * P], g.xT[:, t * P:(t + 1) * P], g.ident[:, :])
                    if t % 4 == 3:
                        mm.then_inc(turned, 1)

            @block.vector
            def _(dve):
                for c in range(NCH):
                    dve.wait_ge(turned, c + 1)
                    dve.tensor_copy(y[:, 4 * c:4 * c + 4, :],
                                    ps[:, c, :].rearrange("p (t d) -> p t d", d=P)).then_inc(copied, 1)

            @block.sync
            def _(sp):
                for c in range(NCH):
                    sp.wait_ge(copied, c + 1)
                    sp.dma_start(dst[:, 4 * c:4 * c + 4, :], y[:, 4 * c:4 * c + 4, :]).then_inc(stored, 16)
                sp.wait_ge(stored, 16 * NCH)


def qkv_stage(nc, g, name, w, vsb, qstk, kstk, rope):
    names = ["wq", "wk", "wv"] + (["wqr", "wkr"] if rope else [])
    with Stage(nc, name) as s:
        wt = {n: s.sb(n, [P, P]) for n in names}
        if rope:
            col = {n: s.sb(n, [P, 1]) for n in ("bq", "bk", "bqr", "bkr")}
            bv = s.sb("bv", [P, P])
            cos, sin = s.sb("cos", [P, SEQ]), s.sb("sin", [P, SEQ])
        flat = {x: s.sb(x + "_flat", [HEADS * 2, TOK], BF16) for x in ("zeros", "ones")}
        t1 = s.sb("t1", [P, 2, 2, CH])
        t2 = s.sb("t2", [P, 2, 2, CH])
        full = s.sb("full", [P, 2, 2, CH])
        rest = s.sb("rest", [P, 2, 2, CH])
        part = [s.sb(f"part{i}", [P, 2, 2, CH], BF16) for i in range(3)]
        ps = s.ps("ps", [P, 8, CH])
        loaded, flat_ready, flat_stored = s.sem("loaded"), s.sem("flat_ready"), s.sem("flat_stored")
        v_ready, v_copied = s.sem("v_ready"), s.sem("v_copied")
        prod, turned, summed = s.sem("prod"), s.sem("turned"), s.sem("summed")
        hi_done, rest_done, mid_done, lo_done = (s.sem(x) for x in ("hi_done", "rest_done", "mid_done", "lo_done"))
        stored = [s.sem(f"stored{u}") for u in range(2)]
        n_load = 0
        with nc.Block() as block:
            loads = [(wt[n][:, :], w[n]) for n in names]
            if rope:
                loads += [(col[n][:, :], w[n]) for n in ("bq", "bk", "bqr", "bkr")]
                loads += [(bv[:, :], w["bv"]), (cos[:, :], w["cos"]), (sin[:, :], w["sin"])]
            n_load = 16 * len(loads)
            per_chunk = 16 * (len(Q_PARTS) + len(K_PARTS))

            @block.gpsimd
            def _(pool):
                pool.memset(flat["zeros"][:, :], 0.0).then_inc(flat_ready, 1)
                pool.memset(flat["ones"][:, :], 1.0).then_inc(flat_ready, 1)
                with pool.Fori(0, NCH // 2) as m:
                    for u in range(2):
                        for x in range(2):
                            k = 4 * m + 2 * u + x
                            if rope:
                                pool.wait_ge(turned, 2 * k + 2)
                                pool.wait_ge(lo_done, 4 * m)
                                pool.tensor_tensor(full[:, u, x, :], t1[:, u, x, :], t2[:, u, x, :],
                                                   ALU.add).then_inc(summed, 1)
                            pool.wait_ge(mid_done, k + 1)
                            pool.tensor_tensor(part[2][:, u, x, :], rest[:, u, x, :], part[1][:, u, x, :],
                                               ALU.subtract).then_inc(lo_done, 1)

            @block.sync
            def _(sp):
                for dst, src in loads:
                    sp.dma_start(dst, src).then_inc(loaded, 16)
                sp.wait_ge(flat_ready, 2)
                for x, stack in (("zeros", qstk), ("ones", kstk)):
                    sp.dma_start(stack[SPECIAL:SPECIAL + 2].rearrange("r h t -> (r h) t"),
                                 flat[x][:, :]).then_inc(flat_stored, 16)
                with sp.Fori(0, NCH // 2) as m:
                    for u in range(2):
                        for x, (stack, parts) in enumerate(((qstk, Q_PARTS), (kstk, K_PARTS))):
                            sp.wait_ge(lo_done, 4 * m + 2 * u + x + 1)
                            for row, p in parts:
                                sp.dma_start(stack[row:row + HD, :, chunk(2 * m + u)].rearrange("r h t -> (r h) t"),
                                             part[p][:, u, x, :]).then_inc(stored[u], 16)
                sp.wait_ge(flat_stored, 32)
                for u in range(2):
                    sp.wait_ge(stored[u], per_chunk * NCH // 2)

            @block.tensor
            def _(pe):
                pe.wait_ge(loaded, n_load)
                for t in range(NT):
                    mm = pe.matmul(ps[:, t // 4, (t % 4) * P:(t % 4 + 1) * P], g.xn[:, t * P:(t + 1) * P],
                                   wt["wv"][:, :], start=True, stop=True)
                    if t % 4 == 3:
                        mm.then_inc(v_ready, 1)
                pe.wait_ge(v_copied, NCH)
                with pe.Fori(0, NCH // 2) as m:
                    for u in range(2):
                        pe.wait_ge(turned, (4 if rope else 2) * 2 * m)
                        for i, n in enumerate(("wq", "wqr", "wk", "wkr") if rope else ("wq", "wk")):
                            pe.matmul(ps[:, 4 * u + i, :], wt[n][:, :], g.xn[:, chunk(2 * m + u)],
                                      start=True, stop=True).then_inc(prod, 1)

            @block.vector
            def _(dve):
                dve.wait_ge(loaded, n_load)
                for c in range(NCH):
                    dve.wait_ge(v_ready, c + 1)
                    o = vsb[:, 4 * c:4 * c + 4, :]
                    i = ps[:, c, :].rearrange("p (t d) -> p t d", d=P)
                    if rope:
                        dve.tensor_tensor(o, i, bv[:, :].unsqueeze(1).to_broadcast([P, 4, P]), ALU.add).then_inc(v_copied, 1)
                    else:
                        dve.tensor_copy(o, i).then_inc(v_copied, 1)
                with dve.Fori(0, NCH // 2) as m:
                    for u in range(2):
                        tok = slice(u * CH, (u + 1) * CH)
                        for x in range(2):
                            k = 4 * m + 2 * u + x
                            if rope:
                                dve.wait_ge(summed, 4 * m)
                                for r, (tt, tab, b) in enumerate(((t1, cos, ("bq", "bk")[x]), (t2, sin, ("bqr", "bkr")[x]))):
                                    dve.wait_ge(prod, 2 * k + r + 1)
                                    dve.scalar_tensor_tensor(out=tt[:, u, x, :], in0=ps[:, 4 * u + 2 * x + r, :],
                                                             scalar=col[b][:, :], in1=tab[:, tok], op0=ALU.add,
                                                             op1=ALU.mult).then_inc(turned, 1)
                            else:
                                dve.wait_ge(prod, k + 1)
                                dve.wait_ge(lo_done, 4 * m)
                                dve.tensor_copy(full[:, u, x, :], ps[:, 4 * u + x, :]).then_inc(turned, 1)
                            dve.wait_ge(hi_done, k + 1)
                            dve.wait_ge(lo_done, 4 * m)
                            dve.tensor_tensor(rest[:, u, x, :], full[:, u, x, :], part[0][:, u, x, :],
                                              ALU.subtract).then_inc(rest_done, 1)

            @block.scalar
            def _(act):
                with act.Fori(0, NCH // 2) as m:
                    for u in range(2):
                        for x in range(2):
                            k = 4 * m + 2 * u + x
                            act.wait_ge(stored[u], per_chunk * m)
                            act.wait_ge(summed if rope else turned, k + 1)
                            act.copy(part[0][:, u, x, :], full[:, u, x, :]).then_inc(hi_done, 1)
                            act.wait_ge(rest_done, k + 1)
                            act.copy(part[1][:, u, x, :], rest[:, u, x, :]).then_inc(mid_done, 1)


def attention_stage(nc, g, name, vsb, qstk, kstk, num, den, scale):
    with Stage(nc, name) as s:
        qst = [s.sb(f"qst{u}", [P, SEQ], BF16) for u in range(4)]
        kst = [[s.sb(f"kst{u}{h}", [P, SEQ], BF16) for h in range(2)] for u in range(4)]
        vst = [s.sb(f"vst{u}", [P, 8, 2, 32]) for u in range(4)]
        pt, warm = s.sb("pt", [P, 4, 2 * CH]), s.sb("warm", [P, 1])
        mx = s.sb("mx", [P, 2, 2, 8, 2])
        nmax = s.sb("nmax", [P, 2, 8])
        mt_in = s.sb("mt_in", [P, 2, 2, 8], BF16)
        mt_out = s.sb("mt_out", [P, 2, 32], BF16)
        oev = s.sb("oev", [P, 2, CH])
        s1 = s.ps("s1", [P, 2, CH])
        st = s.ps("st", [P, 2, 2 * CH])
        av = s.ps("av", [P, 2, CH])
        ldq = [g.ctx.enter_context(nc.semaphore(f"{name}_ldq{u}")) for u in range(4)]
        max_rows = [s.sem(f"max_rows{u}") for u in range(4)]
        max_sent = [s.sem(f"max_sent{u}") for u in range(2)]
        out_done = [s.sem(f"out_done{u}") for u in range(2)]
        turned_max = nc.dram_tensor(f"{name}_turned_max", [4, P, 32], BF16, kind="Internal").ap()
        vset, vcopied, table = s.sem("vset"), s.sem("vcopied"), s.sem("table")
        s1_ready, s1_used = s.sem("s1_ready"), s.sem("s1_used")
        max_step, mt_ready = s.sem("max_step"), s.sem("mt_ready")
        st_ready, exp_done = s.sem("st_ready"), s.sem("exp_done")
        av_ready, evac = s.sem("av_ready"), s.sem("evac")

        with nc.Block() as block:
            @block.gpsimd
            def _(pool):
                for u in range(4):
                    pool.memset(vst[u][:, :, :, :], 0.0).then_inc(vset, 1)
                    pool.memset(qst[u][:, :], 0.0).then_inc(vset, 1)
                    for h in range(2):
                        pool.memset(kst[u][h][:, :], 0.0).then_inc(vset, 1)
                pool.wait_ge(vset, 16)
                for u in range(4):
                    pool.memset(vst[u][:, :, :, HD:2 * HD], 1.0).then_inc(vset, 1)
                pool.wait_ge(vset, 20)

                def fetch(b, hp, after):
                    u = hp % 4
                    if after is not None:
                        pool.wait_ge(av_ready, after)
                    for h in range(2):
                        for t, src in ((qst[u], qstk), (kst[u][h], kstk)):
                            pool.dma_start(t[64 * h:64 * h + STACK, :],
                                           src[:, 2 * hp + h, bass.ds(b * SEQ, SEQ)]).then_inc(ldq[u], 16)
                    vcopy = vsb[:, bass.ds(b * 8, 8), 16 * hp:16 * hp + 16].rearrange("p k (h d) -> p k h d", d=HD)
                    pool.tensor_copy(vst[u][:, :, :, 0:HD], vcopy).then_inc(vcopied, 1)

                for hp in range(PAIRS):
                    fetch(0, hp, hp - 3 if hp >= 4 else None)
                with pool.Fori(1, BATCH) as b:
                    for hp in range(PAIRS):
                        fetch(b, hp, PAIRS * b + hp - 3)

            @block.sync
            def _(sp):
                def rows(n, u, sent):
                    sp.wait_ge(mt_ready, n + 1)
                    sp.dma_start(turned_max[u % 4], mt_out[:, u % 2, :]).then_inc(max_sent[u % 2], 16)
                    sp.wait_ge(max_sent[u % 2], sent)
                    for h in range(2):
                        sp.dma_start(qst[u % 4][64 * h + SPECIAL:64 * h + SPECIAL + 2, :].rearrange(
                                         "x (k p q) -> x k p q", p=4, q=32),
                                     turned_max[u % 4].rearrange("(p h x k) q -> h x k p q", p=4, h=2, x=2)[h]
                                     ).then_inc(max_rows[u % 4], 16)

                def result(b, hp):
                    sp.wait_ge(evac, PAIRS * b + hp + 1)
                    for gr in range(4):
                        r = (2 * hp + gr // 2) * HD
                        sp.dma_start(num[r:r + HD, chunk(2 * b + gr % 2)],
                                     oev[32 * gr:32 * gr + HD, hp % 2, :]).then_inc(out_done[hp % 2], 16)
                    sp.dma_start(den[bass.ds(4 * (PAIRS * b + hp), 4), :],
                                 oev[HD:P:32, hp % 2, :]).then_inc(out_done[hp % 2], 16)

                for n in range(3):
                    rows(n, n, 16 * (n // 2 + 1))
                with sp.Fori(0, BATCH - 1) as b:
                    for hp in range(PAIRS):
                        result(b, hp)
                        rows(PAIRS * b + hp + 3, hp + 3, 16 * (PAIRS // 2 * b + (hp + 3) // 2 + 1))
                for hp in range(PAIRS):
                    result(BATCH - 1, hp)
                    if hp + 3 < PAIRS:
                        rows(NPAIR - PAIRS + hp + 3, hp + 3, 16 * ((NPAIR - PAIRS + hp + 3) // 2 + 1))
                for u in range(2):
                    sp.wait_ge(out_done[u], 80 * NPAIR // 2)

            @block.tensor
            def _(pe):
                def first_unit(n, u, rounds, j):
                    qt, kh, h = j // 4, (j // 2) % 2, j % 2
                    if j == 0:
                        pe.wait_ge(ldq[u], 64 * rounds)
                    if not (isinstance(n, int) and 32 * n + j < 2):
                        pe.wait_ge(s1_used, 32 * n + j - 1)
                    pe.matmul(s1[:, j % 2, :], qst[u][:, qt * P:(qt + 1) * P], kst[u][h][:, kh * CH:(kh + 1) * CH],
                              start=True, stop=True).then_inc(s1_ready, 1)

                def weigh(n, u, i):
                    kt = i // 2
                    if i == 0:
                        pe.wait_ge(vcopied, n + 1)
                        if not (isinstance(n, int) and n < 2):
                            pe.wait_ge(evac, n - 1)
                    pe.wait_ge(exp_done, 16 * n + i + 2)
                    for half in range(2):
                        for h in range(2):
                            gr = 2 * h + half
                            mm = pe.matmul(av[32 * gr:32 * gr + 32, u % 2, :], vst[u][:, kt, h, :],
                                           pt[:, (i + half) % 4, h * CH:(h + 1) * CH], start=kt == 0, stop=kt == 7)
                    if i == 14:
                        mm.then_inc(av_ready, 1)

                def pair(m, u, first, before):
                    n = 4 * m + u
                    pe.wait_ge(max_rows[u], 32 * (m + 1))
                    for i in range(0, 16, 2):
                        kt = i // 2
                        for half in range(2):
                            if not (i == 0 and not before):
                                pe.wait_ge(exp_done, 16 * n + i - 1 + half)
                            for h in range(2):
                                mm = pe.matmul(st[:, half, h * CH:(h + 1) * CH], kst[u][h][:, kt * P:(kt + 1) * P],
                                               qst[u][:, half * CH:(half + 1) * CH], start=True, stop=True)
                            mm.then_inc(st_ready, 1)
                            if first:
                                first_unit(n + 2, (u + 2) % 4, m + 1 + (u >= 2), 2 * i + half)
                        if i >= 2:
                            weigh(n, u, i - 2)
                        elif before:
                            weigh(n - 1, (u + 3) % 4, 14)
                        if first:
                            for j in range(2 * i + 2, 2 * i + 4):
                                first_unit(n + 2, (u + 2) % 4, m + 1 + (u >= 2), j)

                for n in range(2):
                    for j in range(32):
                        first_unit(n, n, 1, j)
                for u in range(4):
                    pair(0, u, True, u > 0)
                with pe.Fori(1, NPAIR // 4 - 1) as m:
                    for u in range(4):
                        pair(m, u, True, True)
                for u in range(4):
                    pair(NPAIR // 4 - 1, u, u < 2, True)
                weigh(NPAIR - 1, 3, 14)

            @block.scalar
            def _(act):
                act.activation(warm[:, :], g.eps[:, :], ACT.Exp).then_inc(table, 1)
                with act.Fori(0, NPAIR) as n:
                    for i in range(16):
                        act.wait_ge(st_ready, 16 * n + i + 1)
                        act.activation(pt[:, i % 4, :], st[:, i % 2, :], ACT.Exp, scale=scale).then_inc(exp_done, 1)

            @block.vector
            def _(dve):
                def reduce_units(n, par, lo, hi):
                    for j in range(lo, hi):
                        qt, kh, h = j // 4, (j // 2) % 2, j % 2
                        dve.wait_ge(s1_ready, 32 * n + j + 1)
                        dve.tensor_reduce(mx[:, par, h, qt, kh:kh + 1], s1[:, j % 2, :], AX.X, ALU.max).then_inc(s1_used, 1)

                def finish_max(n, par, rows_of, rows_out):
                    dve.wait_ge(s1_used, 32 * (n + 1))
                    if rows_of is not None:
                        dve.wait_ge(rows_of, rows_out)
                    dve.tensor_reduce(nmax[:, :, :], mx[:, par], AX.X, ALU.max, negate=True).then_inc(max_step, 1)
                    dve.wait_ge(max_step, 3 * n + 1)
                    dve.tensor_copy(mt_in[:, :, 0, :], nmax[:, :, :]).then_inc(max_step, 1)
                    dve.wait_ge(max_step, 3 * n + 2)
                    dve.tensor_tensor(mt_in[:, :, 1, :], nmax[:, :, :], mt_in[:, :, 0, :], ALU.subtract).then_inc(max_step, 1)
                    dve.wait_ge(max_step, 3 * n + 3)
                    dve.transpose(mt_out[:, par, :], mt_in[:, :, :, :].rearrange("p h x k -> p (h x k)")).then_inc(mt_ready, 1)

                def sums(m, u):
                    dve.wait_ge(av_ready, 4 * m + u + 1)
                    dve.wait_ge(out_done[u % 2], 80 * (2 * m + u // 2))
                    dve.tensor_copy(oev[:, u % 2, :], av[:, u % 2, :]).then_inc(evac, 1)

                for n in range(2):
                    reduce_units(n, n, 0, 32)
                    finish_max(n, n, None, None)

                def step(m, u, maxima, before):
                    n = 4 * m + u
                    if maxima:
                        reduce_units(n + 2, u % 2, 0, 12)
                    if before:
                        sums(m - (u == 0), (u + 3) % 4)
                    if maxima:
                        reduce_units(n + 2, u % 2, 12, 32)
                        finish_max(n + 2, u % 2, max_sent[u % 2], 16 * (2 * m + u // 2 + 1))

                for u in range(4):
                    step(0, u, True, u > 0)
                with dve.Fori(1, NPAIR // 4 - 1) as m:
                    for u in range(4):
                        step(m, u, True, True)
                for u in range(4):
                    step(NPAIR // 4 - 1, u, u < 2, True)
                sums(NPAIR // 4 - 1, 3)


def out_proj_stage(nc, g, name, wo_dram, bo_dram, num, den, rden, factor):
    with Stage(nc, name) as s:
        wo, bo = s.sb("wo", [P, P]), s.sb("bo", [P, 1])
        dn, rd = s.sb("dn", [P, CH]), s.sb("rd", [P, CH])
        nm, rb, cx = s.sb("nm", [P, 2, CH]), s.sb("rb", [P, 2, CH]), s.sb("cx", [P, 2, CH])
        ps = s.ps("ps", [P, 2, CH])
        wl, dl, rdone, rstore = s.sem("wl"), s.sem("dl"), s.sem("rdone"), s.sem("rstore")
        cl = [s.sem(f"cl{u}") for u in range(2)]
        ctx_ready, proj_ready, added = s.sem("ctx_ready"), s.sem("proj_ready"), s.sem("added")
        by_chunk = rden.rearrange("(b h f) t -> b f h t", b=BATCH, f=2)
        with nc.Block() as block:
            @block.sync
            def _(sp):
                sp.dma_start(dn[:, :], den).then_inc(dl, 16)
                sp.dma_start(wo[:, :], wo_dram).then_inc(wl, 16)
                if bo_dram is not None:
                    sp.dma_start(bo[:, :], bo_dram).then_inc(wl, 16)
                sp.wait_ge(rdone, 1)
                sp.dma_start(rden, rd[:, :]).then_inc(rstore, 16)
                sp.wait_ge(rstore, 16)
                with sp.Fori(0, NCH // 2) as m:
                    for u in range(2):
                        sp.wait_ge(ctx_ready, 2 * m)
                        sp.dma_start(nm[:, u, :], num[:, chunk(2 * m + u)]).then_inc(cl[u], 16)
                        sp.dma_start(rb[:, u, :], by_chunk[m, u].unsqueeze(1).to_broadcast([HEADS, HD, CH])
                                     ).then_inc(cl[u], 16)

            @block.vector
            def _(dve):
                dve.wait_ge(dl, 16)
                dve.reciprocal(rd[:, :], dn[:, :]).then_inc(rdone, 1)
                dve.wait_ge(wl, 16 if bo_dram is None else 32)
                with dve.Fori(0, NCH // 2) as m:
                    for u in range(2):
                        c = 2 * m + u
                        dve.wait_ge(cl[u], 32 * (m + 1))
                        dve.wait_ge(proj_ready, 2 * m)
                        dve.tensor_tensor(cx[:, u, :], nm[:, u, :], rb[:, u, :], ALU.mult).then_inc(ctx_ready, 1)
                        dve.wait_ge(proj_ready, c + 1)
                        if bo_dram is None:
                            dve.scalar_tensor_tensor(out=g.xT[:, chunk(c)], in0=ps[:, u, :], scalar=factor,
                                                     in1=g.xT[:, chunk(c)], op0=ALU.mult, op1=ALU.add).then_inc(added, 1)
                        else:
                            dve.scalar_tensor_tensor(out=g.xT[:, chunk(c)], in0=ps[:, u, :], scalar=bo[:, :],
                                                     in1=g.xT[:, chunk(c)], op0=ALU.add, op1=ALU.add).then_inc(added, 1)
                dve.wait_ge(added, NCH)

            @block.tensor
            def _(pe):
                pe.wait_ge(wl, 16 if bo_dram is None else 32)
                with pe.Fori(0, NCH // 2) as m:
                    for u in range(2):
                        pe.wait_ge(ctx_ready, 2 * m + u + 1)
                        pe.wait_ge(added, 2 * m)
                        pe.matmul(ps[:, u, :], wo[:, :], cx[:, u, :], start=True, stop=True).then_inc(proj_ready, 1)


def attention(nc, g, name, w, rope, scale, bo, factor):
    qstk = nc.dram_tensor(f"{name}_qstk", [STACK, HEADS, TOK], BF16, kind="Internal").ap()
    kstk = nc.dram_tensor(f"{name}_kstk", [STACK, HEADS, TOK], BF16, kind="Internal").ap()
    num = nc.dram_tensor(f"{name}_num", [P, TOK], F32, kind="Internal").ap()
    den = nc.dram_tensor(f"{name}_den", [NPAIR * 4, CH], F32, kind="Internal").ap()
    rden = nc.dram_tensor(f"{name}_rden", [NPAIR * 4, CH], F32, kind="Internal").ap()
    with nc.sbuf_tensor(f"{name}_v", [P, NT, P], F32) as vsb:
        qkv_stage(nc, g, name + "_qkv", w, vsb, qstk, kstk, rope)
        attention_stage(nc, g, name + "_att", vsb, qstk, kstk, num, den, scale)
    out_proj_stage(nc, g, name + "_out", w["wo"], bo, num, den, rden, factor)


class Globals:
    pass


def first_max(dve, link, L, m, oh, desc, rows, e):
    wide = [P, NT, e]
    link(dve.tensor_reduce(m, L, AX.X, ALU.max))
    link(dve.tensor_tensor(oh, L, m.unsqueeze(2).to_broadcast(wide), ALU.is_equal))
    link(dve.tensor_tensor(oh, oh, desc.unsqueeze(1).to_broadcast(wide), ALU.mult))
    link(dve.tensor_reduce(rows, oh, AX.X, ALU.max))
    link(dve.tensor_tensor(oh, oh, rows.unsqueeze(2).to_broadcast(wide), ALU.is_equal))


def logits_of(pe, g, s_ps, gate, e):
    for t in range(NT):
        mm = pe.matmul(s_ps[:, t * e:(t + 1) * e], g.xn[:, t * P:(t + 1) * P], gate[:, :], start=True, stop=True)
    return mm


def turn_parts(pe, parts, ident_b, tps, rows, split_done, steps, copied, turned_sem):
    pe.wait_ge(split_done, steps)
    for t in range(NT):
        if t % 4 == 0 and t >= 16:
            pe.wait_ge(copied, t // 4 - 3)
        mm = pe.matmul(tps[0:rows, (t // 4) % 4, (t % 4) * P:(t % 4 + 1) * P], parts[:, t, :], ident_b[:, :],
                       start=True, stop=True)
        if t % 4 == 3:
            mm.then_inc(turned_sem, 1)


def top2_stage(nc, g, name, gate_dram, desc_dram, combT, e, over_all):
    rows = 3 * (e + 1)
    wide = [P, NT, e]
    with Stage(nc, name) as s:
        gate, desc = s.sb("gate", [P, e]), s.sb("desc", [P, e])
        L, ex, oh1, oh2 = (s.sb(x, wide) for x in ("L", "ex", "oh1", "oh2"))
        m1, m2, w1, w2, tmp = (s.sb(x, [P, NT]) for x in ("m1", "m2", "w1", "w2", "tmp"))
        comb = s.sb("comb", [P, NT, e + 1])
        parts = s.sb("parts", [P, NT, rows], BF16)
        ps = s.ps("ps", [P, NT * e])
        tps = s.ps("tps", [P, 4, CH])
        loaded, logits, step, turned, copied = (s.sem(x) for x in ("loaded", "logits", "step", "turned", "copied"))
        diff_ready, exp_ready, split_done = s.sem("diff_ready"), s.sem("exp_ready"), s.sem("split_done")
        with nc.Block() as block:
            @block.sync
            def _(sp):
                sp.dma_start(gate[:, :], gate_dram).then_inc(loaded, 16)
                sp.dma_start(desc[:, :], desc_dram).then_inc(loaded, 16)

            @block.tensor
            def _(pe):
                pe.wait_ge(loaded, 32)
                logits_of(pe, g, ps, gate, e).then_inc(logits, 1)
                turn_parts(pe, parts, g.ident_b, tps, rows, split_done, 1, copied, turned)

            @block.vector
            def _(dve):
                n = [0]

                def link(ins):
                    n[0] += 1
                    ins.then_inc(step, 1)
                    dve.wait_ge(step, n[0])

                dve.wait_ge(loaded, 32)
                dve.wait_ge(logits, 1)
                link(dve.tensor_copy(L[:, :, :], ps[:, :].rearrange("p (t e) -> p t e", e=e)))
                first_max(dve, link, L[:, :, :], m1[:, :], oh1[:, :, :], desc[:, :], tmp[:, :], e)
                link(dve.scalar_tensor_tensor(out=ex[:, :, :], in0=oh1[:, :, :], scalar=-1e30, in1=L[:, :, :],
                                              op0=ALU.mult, op1=ALU.add))
                first_max(dve, link, ex[:, :, :], m2[:, :], oh2[:, :, :], desc[:, :], tmp[:, :], e)
                dve.tensor_tensor(m2[:, :], m2[:, :], m1[:, :], ALU.subtract).then_inc(diff_ready, 1)
                if over_all:
                    dve.tensor_tensor(ex[:, :, :], L[:, :, :], m1[:, :].unsqueeze(2).to_broadcast(wide),
                                      ALU.subtract).then_inc(diff_ready, 1)
                dve.wait_ge(exp_ready, 1)
                if over_all:
                    link(dve.tensor_reduce(tmp[:, :], ex[:, :, :], AX.X, ALU.add))
                else:
                    link(dve.tensor_scalar(tmp[:, :], w2[:, :], 1.0, None, ALU.add))
                link(dve.reciprocal(w1[:, :], tmp[:, :]))
                link(dve.tensor_tensor(w2[:, :], w2[:, :], w1[:, :], ALU.mult))
                link(dve.tensor_tensor(oh1[:, :, :], oh1[:, :, :], w1[:, :].unsqueeze(2).to_broadcast(wide), ALU.mult))
                link(dve.tensor_tensor(oh2[:, :, :], oh2[:, :, :], w2[:, :].unsqueeze(2).to_broadcast(wide), ALU.mult))
                link(dve.memset(comb[:, :, e:e + 1], 1.0))
                link(dve.tensor_tensor(comb[:, :, 0:e], oh1[:, :, :], oh2[:, :, :], ALU.add))
                hi, mid, lo = (parts[:, :, i * (e + 1):(i + 1) * (e + 1)] for i in range(3))
                link(dve.tensor_copy(hi, comb[:, :, :]))
                link(dve.tensor_tensor(comb[:, :, :], comb[:, :, :], hi, ALU.subtract))
                link(dve.tensor_copy(mid, comb[:, :, :]))
                dve.tensor_tensor(lo, comb[:, :, :], mid, ALU.subtract).then_inc(split_done, 1)
                for c in range(NCH):
                    dve.wait_ge(turned, c + 1)
                    dve.tensor_copy(combT[0:rows, c * CH:(c + 1) * CH], tps[0:rows, c % 4, :]).then_inc(copied, 1)
                dve.wait_ge(copied, NCH)

            @block.scalar
            def _(act):
                act.wait_ge(diff_ready, 2 if over_all else 1)
                if over_all:
                    act.activation(w2[:, :], m2[:, :], ACT.Exp)
                    act.activation(ex[:, :, :], ex[:, :, :], ACT.Exp).then_inc(exp_ready, 1)
                else:
                    act.activation(w2[:, :], m2[:, :], ACT.Exp).then_inc(exp_ready, 1)


def glu_stage(nc, g, name, tiles, w, combT, rows):
    with Stage(nc, name) as s:
        wg, wu, wd = (s.sb(x, [P, tiles, P]) for x in ("wg", "wu", "wd"))
        self_, sel = s.sb("self", [rows, tiles, P]), s.sb("sel", [rows, tiles, P], BF16)
        sg, h1, h = s.sb("sg", [P, 2, CH]), s.sb("h1", [P, 2, CH]), s.sb("h", [P, 3, CH])
        gp, up, cp, yp = (s.ps(x, [P, 2, CH]) for x in ("gp", "up", "cp", "yp"))
        loaded, sel_in, sel_ready = s.sem("loaded"), s.sem("sel_in"), s.sem("sel_ready")
        gu_ready, silu_done, h1_done, h_done = (s.sem(x) for x in ("gu_ready", "silu_done", "h1_done", "h_done"))
        y_ready, y_added = s.sem("y_ready"), s.sem("y_added")
        body = 2 * tiles
        with nc.Block() as block:
            @block.sync
            def _(sp):
                sp.dma_start(self_[:, :, :], w["sel"]).then_inc(sel_in, 16)
                for t, n in ((wg, "wg"), (wu, "wu"), (wd, "wd")):
                    sp.dma_start(t[:, :, :], w[n]).then_inc(loaded, 16)

            @block.gpsimd
            def _(pool):
                pool.wait_ge(sel_in, 16)
                pool.tensor_copy(sel[:, :, :], self_[:, :, :]).then_inc(sel_ready, 1)

            @block.tensor
            def _(pe):
                pe.wait_ge(loaded, 48)
                pe.wait_ge(sel_ready, 1)
                with pe.Fori(0, NCH // 2) as m:
                    def down(j):
                        u, t = j // tiles, j % tiles
                        if t == 0:
                            pe.wait_ge(y_added, 2 * m)
                        pe.wait_ge(h_done, body * m + j + 1)
                        mm = pe.matmul(yp[:, u, :], wd[:, t, :], h[:, j % 3, :], start=t == 0, stop=t == tiles - 1)
                        if t == tiles - 1:
                            mm.then_inc(y_ready, 1)

                    for j in range(body):
                        u, t = j // tiles, j % tiles
                        x = g.xn[:, chunk(2 * m + u)]
                        pe.matmul(gp[:, j % 2, :], wg[:, t, :], x, start=True, stop=True)
                        pe.matmul(up[:, j % 2, :], wu[:, t, :], x, start=True, stop=True)
                        pe.matmul(cp[:, j % 2, :], sel[:, t, :], combT[0:rows, chunk(2 * m + u)],
                                  start=True, stop=True).then_inc(gu_ready, 1)
                        if j >= 1:
                            down(j - 1)
                    down(body - 1)

            @block.scalar
            def _(act):
                with act.Fori(0, NCH // 2) as m:
                    for j in range(body):
                        act.wait_ge(gu_ready, body * m + j + 1)
                        act.activation(sg[:, j % 2, :], gp[:, j % 2, :], ACT.Silu).then_inc(silu_done, 1)

            @block.vector
            def _(dve):
                with dve.Fori(0, NCH // 2) as m:
                    def add_y(u):
                        c = 2 * m + u
                        dve.wait_ge(y_ready, c + 1)
                        dve.tensor_tensor(g.xT[:, chunk(c)], g.xT[:, chunk(c)], yp[:, u, :], ALU.add).then_inc(y_added, 1)

                    for j in range(body):
                        dve.wait_ge(silu_done, body * m + j + 1)
                        dve.tensor_tensor(h1[:, j % 2, :], sg[:, j % 2, :], up[:, j % 2, :], ALU.mult).then_inc(h1_done, 1)
                        dve.wait_ge(h1_done, body * m + j + 1)
                        dve.tensor_tensor(h[:, j % 3, :], h1[:, j % 2, :], cp[:, j % 2, :], ALU.mult).then_inc(h_done, 1)
                        if j == tiles + 3:
                            add_y(0)
                    add_y(1)
                dve.wait_ge(y_added, NCH)


CAPACITY = 640


def top1_stage(nc, g, name, w, maskT, maskT_b):
    e, bits = 8, 28
    wide = [P, NT, e]
    with Stage(nc, name) as s:
        gate, desc, before_w = s.sb("gate", [P, e]), s.sb("desc", [P, e]), s.sb("before_w", [P, P])
        L, ex, oh, pm, t1, t2, eq = (s.sb(x, wide) for x in ("L", "ex", "oh", "pm", "t1", "t2", "eq"))
        m1, tmp, p1 = (s.sb(x, [P, NT]) for x in ("m1", "tmp", "p1"))
        thr, cand, part, inc = (s.sb(x, [P, e]) for x in ("thr", "cand", "part", "inc"))
        fin = s.sb("fin", wide, BF16)
        ps = s.ps("ps", [P, NT * e])
        cnt_ps, pre_ps, tot_ps = s.ps("cnt", [P, e]), s.ps("pre", [P, NT * e]), s.ps("tot", [P, NT * e])
        tps = s.ps("tps", [P, 4, CH])
        loaded, logits, step, turned, copied = (s.sem(x) for x in ("loaded", "logits", "step", "turned", "copied"))
        diff_ready, exp_ready, fin_done = s.sem("diff_ready"), s.sem("exp_ready"), s.sem("fin_done")
        counted_here, counted, thr_done = s.sem("counted_here"), s.sem("counted"), s.sem("thr_done")
        eq_ready, prefix_ready = s.sem("eq_ready"), s.sem("prefix_ready")
        cand_done, cmp_done, acc_done = s.sem("cand_done"), s.sem("cmp_done"), s.sem("acc_done")
        with nc.Block() as block:
            @block.sync
            def _(sp):
                for d, n in ((gate, "gate"), (desc, "desc"), (before_w, "before")):
                    sp.dma_start(d[:, :], w[n]).then_inc(loaded, 16)

            @block.tensor
            def _(pe):
                pe.wait_ge(loaded, 48)
                logits_of(pe, g, ps, gate, e).then_inc(logits, 1)
                with pe.Fori(0, bits + 1) as k:
                    pe.wait_ge(counted_here, k + 1)
                    pe.matmul(cnt_ps[:, :], g.ones[:, :], part[:, :], start=True, stop=True).then_inc(counted, 1)
                pe.wait_ge(eq_ready, 1)
                flat = eq[:, :, :].rearrange("p t e -> p (t e)")
                pe.matmul(pre_ps[:, :], before_w[:, :], flat, start=True, stop=True)
                pe.matmul(tot_ps[:, :], g.ones[:, :], flat, start=True, stop=True).then_inc(prefix_ready, 1)
                turn_parts(pe, fin, g.ident_b, tps, e, fin_done, 1, copied, turned)

            @block.vector
            def _(dve):
                n = [0]

                def link(ins):
                    n[0] += 1
                    ins.then_inc(step, 1)
                    dve.wait_ge(step, n[0])

                over_tiles = lambda t: t[:, :, :].rearrange("p t e -> p e t")
                wide_e = lambda t: t.unsqueeze(1).to_broadcast(wide)
                dve.wait_ge(loaded, 48)
                dve.wait_ge(logits, 1)
                link(dve.tensor_copy(L[:, :, :], ps[:, :].rearrange("p (t e) -> p t e", e=e)))
                first_max(dve, link, L[:, :, :], m1[:, :], oh[:, :, :], desc[:, :], tmp[:, :], e)
                dve.tensor_tensor(ex[:, :, :], L[:, :, :], m1[:, :].unsqueeze(2).to_broadcast(wide),
                                  ALU.subtract).then_inc(diff_ready, 1)
                dve.wait_ge(exp_ready, 1)
                link(dve.tensor_reduce(tmp[:, :], ex[:, :, :], AX.X, ALU.add))
                link(dve.reciprocal(p1[:, :], tmp[:, :]))
                link(dve.tensor_tensor(pm[:, :, :], oh[:, :, :], p1[:, :].unsqueeze(2).to_broadcast(wide), ALU.mult))
                link(dve.memset(thr[:, :], 0.0))
                link(dve.memset(inc[:, :], 0.5))
                with dve.Fori(0, bits) as k:
                    dve.tensor_tensor(cand[:, :], thr[:, :], inc[:, :], ALU.add).then_inc(cand_done, 1)
                    dve.wait_ge(cand_done, k + 1)
                    dve.tensor_tensor(t1[:, :, :], pm[:, :, :], wide_e(cand[:, :]), ALU.is_ge).then_inc(cmp_done, 1)
                    dve.wait_ge(cmp_done, k + 1)
                    dve.tensor_reduce(part[:, :], over_tiles(t1), AX.X, ALU.add).then_inc(counted_here, 1)
                    dve.wait_ge(counted, k + 1)
                    dve.scalar_tensor_tensor(out=cand[:, :], in0=cnt_ps[:, :], scalar=CAPACITY - 0.5, in1=inc[:, :],
                                             op0=ALU.is_gt, op1=ALU.mult).then_inc(acc_done, 1)
                    dve.wait_ge(acc_done, k + 1)
                    dve.tensor_scalar(inc[:, :], inc[:, :], 0.5, None, ALU.mult)
                    dve.tensor_tensor(thr[:, :], thr[:, :], cand[:, :], ALU.add).then_inc(thr_done, 1)
                    dve.wait_ge(thr_done, k + 1)
                link(dve.tensor_tensor(t1[:, :, :], pm[:, :, :], wide_e(thr[:, :]), ALU.is_gt))
                dve.tensor_reduce(part[:, :], over_tiles(t1), AX.X, ALU.add).then_inc(counted_here, 1)
                link(dve.tensor_tensor(t2[:, :, :], pm[:, :, :], wide_e(thr[:, :]), ALU.is_equal))
                dve.tensor_tensor(eq[:, :, :], t2[:, :, :], oh[:, :, :], ALU.mult).then_inc(eq_ready, 1)
                dve.wait_ge(counted, bits + 1)
                link(dve.tensor_scalar(cand[:, :], cnt_ps[:, :], -1.0, float(CAPACITY), ALU.mult, ALU.add))
                dve.wait_ge(prefix_ready, 1)
                dve.wait_ge(eq_ready, 1)
                link(dve.tensor_copy(ex[:, :, :], tot_ps[:, :].rearrange("p (t e) -> p t e", e=e)))
                for i in range(e):
                    last = dve.tensor_tensor_scan(t2[:, :, i], g.ones[:, 0:NT], ex[:, :, i], 0.0, ALU.mult, ALU.add)
                link(last)
                link(dve.tensor_tensor(t2[:, :, :], t2[:, :, :], ex[:, :, :], ALU.subtract))
                link(dve.tensor_tensor(t2[:, :, :], t2[:, :, :], pre_ps[:, :].rearrange("p (t e) -> p t e", e=e), ALU.add))
                link(dve.tensor_tensor(t2[:, :, :], t2[:, :, :], wide_e(cand[:, :]), ALU.is_lt))
                link(dve.tensor_tensor(t2[:, :, :], t2[:, :, :], eq[:, :, :], ALU.mult))
                link(dve.tensor_tensor(t1[:, :, :], t1[:, :, :], t2[:, :, :], ALU.add))
                link(dve.tensor_reduce(tmp[:, :], t1[:, :, :], AX.X, ALU.add))
                link(dve.tensor_scalar(tmp[:, :], tmp[:, :], -1.0, 1.0, ALU.mult, ALU.add))
                link(dve.tensor_tensor(t1[:, :, 0], t1[:, :, 0], tmp[:, :], ALU.add))
                dve.tensor_copy(fin[:, :, :], t1[:, :, :]).then_inc(fin_done, 1)
                for c in range(NCH):
                    dve.wait_ge(turned, c + 1)
                    dve.tensor_copy(maskT[:, c * CH:(c + 1) * CH], tps[0:e, c % 4, :])
                    dve.tensor_copy(maskT_b[:, c * CH:(c + 1) * CH], tps[0:e, c % 4, :]).then_inc(copied, 1)
                dve.wait_ge(copied, NCH)

            @block.scalar
            def _(act):
                act.wait_ge(diff_ready, 1)
                act.activation(ex[:, :, :], ex[:, :, :], ACT.Exp).then_inc(exp_ready, 1)


def expert_stage(nc, g, name, w, maskT, maskT_b):
    e, per = 8, 4
    tiles = e * per
    with Stage(nc, name) as s:
        w1, w2 = s.sb("w1", [P, tiles, P]), s.sb("w2", [P, tiles, P])
        b1, b2 = s.sb("b1", [P, tiles]), s.sb("b2", [e, P])
        self_, sel = s.sb("self", [e, e, P]), s.sb("sel", [e, e, P], BF16)
        r, h = s.sb("r", [P, 3, CH]), s.sb("h", [P, 3, CH])
        zp, mp, yp = s.ps("zp", [P, 3, CH]), s.ps("mp", [P, 2, CH]), s.ps("yp", [P, 2, CH])
        small_in, w1_in, w2_in, sel_ready = s.sem("small_in"), s.sem("w1_in"), s.sem("w2_in"), s.sem("sel_ready")
        z_ready, relu_done, h_done = s.sem("z_ready"), s.sem("relu_done"), s.sem("h_done")
        y_ready, y_added = s.sem("y_ready"), s.sem("y_added")
        body = 2 * tiles
        with nc.Block() as block:
            @block.sync
            def _(sp):
                for d, n in ((self_, "sel"), (b1, "b1"), (b2, "b2")):
                    sp.dma_start(d[...], w[n]).then_inc(small_in, 16)
                sp.dma_start(w1[...], w["w1"]).then_inc(w1_in, 16)
                sp.dma_start(w2[...], w["w2"]).then_inc(w2_in, 16)

            @block.gpsimd
            def _(pool):
                pool.wait_ge(small_in, 48)
                pool.tensor_copy(sel[:, :, :], self_[:, :, :]).then_inc(sel_ready, 1)

            @block.tensor
            def _(pe):
                pe.wait_ge(sel_ready, 1)
                pe.wait_ge(w1_in, 16)
                pe.wait_ge(w2_in, 16)
                with pe.Fori(0, NCH // 2) as m:
                    def down(j):
                        u, t = j // tiles, j % tiles
                        if t == 0:
                            pe.wait_ge(y_added, 2 * m)
                            pe.matmul(yp[:, u, :], b2[:, :], maskT[:, chunk(2 * m + u)], start=True, stop=False)
                        pe.wait_ge(h_done, body * m + j + 1)
                        mm = pe.matmul(yp[:, u, :], w2[:, t, :], h[:, j % 3, :], start=False, stop=t == tiles - 1)
                        if t == tiles - 1:
                            mm.then_inc(y_ready, 1)

                    for j in range(body):
                        u, t = j // tiles, j % tiles
                        if t % per == 0:
                            pe.matmul(mp[:, (j // per) % 2, :], sel[:, t // per, :], maskT_b[:, chunk(2 * m + u)],
                                      start=True, stop=True)
                        pe.matmul(zp[:, j % 2, :], w1[:, t, :], g.xn[:, chunk(2 * m + u)],
                                  start=True, stop=True).then_inc(z_ready, 1)
                        if j >= 1:
                            down(j - 1)
                    down(body - 1)

            @block.scalar
            def _(act):
                act.wait_ge(small_in, 48)
                with act.Fori(0, NCH // 2) as m:
                    for j in range(body):
                        act.wait_ge(z_ready, body * m + j + 1)
                        act.activation(r[:, j % 2, :], zp[:, j % 2, :], ACT.Relu,
                                       bias=b1[:, j % tiles:j % tiles + 1]).then_inc(relu_done, 1)

            @block.vector
            def _(dve):
                with dve.Fori(0, NCH // 2) as m:
                    def add_y(u):
                        c = 2 * m + u
                        dve.wait_ge(y_ready, c + 1)
                        dve.tensor_tensor(g.xT[:, chunk(c)], g.xT[:, chunk(c)], yp[:, u, :], ALU.add).then_inc(y_added, 1)

                    for j in range(body):
                        dve.wait_ge(relu_done, body * m + j + 1)
                        dve.tensor_tensor(h[:, j % 3, :], r[:, j % 2, :], mp[:, (j // per) % 2, :], ALU.mult).then_inc(h_done, 1)
                        if j == tiles + 3:
                            add_y(0)
                    add_y(1)
                dve.wait_ge(y_added, NCH)


def conv_in_stage(nc, g, name, w, xs, z_dram, z_func, b0):
    with Stage(nc, name) as s:
        win, wb0 = s.sb("win", [P, 4, P]), s.sb("wb0", [P, P])
        cw, cb = s.sb("cw", [P, 2, 4]), s.sb("cb", [P, 2])
        xb = s.sb("xb", [P, 2, BATCH, SEQ + 3])
        acc = s.sb("acc", [P, 2, 4, CH])
        zt = s.sb("zt", [P, 2, 2, CH])
        ps, bps = s.ps("ps", [P, 6, CH]), s.ps("bps", [P, 2, CH])
        loaded, padded, prod, b0_prod = (s.sem(x) for x in ("loaded", "padded", "prod", "b0_prod"))
        xb_done, tap, z_done, silu_done, b0_done = (s.sem(x) for x in ("xb_done", "tap", "z_done", "silu_done", "b0_done"))
        z_stored = [s.sem(f"z_stored{u}") for u in range(2)]
        loads = [(win, "win"), (cw, "cw"), (cb, "cb")] + ([(wb0, "wb0")] if b0 is not None else [])
        zs = z_dram.rearrange("(x p) t -> p x t", p=P)
        with nc.Block() as block:
            @block.sync
            def _(sp):
                for d, n in loads:
                    sp.dma_start(d[...], w[n]).then_inc(loaded, 16)
                with sp.Fori(0, BATCH) as b:
                    for u in range(2):
                        sp.wait_ge(z_done, 4 * b + 2 * u + 2)
                        sp.dma_start(zs[:, :, chunk(2 * b + u)], zt[:, u, :, :]).then_inc(z_stored[u], 16)
                for u in range(2):
                    sp.wait_ge(z_stored[u], 16 * BATCH)

            @block.gpsimd
            def _(pool):
                pool.memset(xb[:, :, :, 0:3], 0.0).then_inc(padded, 1)

            @block.tensor
            def _(pe):
                pe.wait_ge(loaded, 16 * len(loads))
                with pe.Fori(0, BATCH) as b:
                    for u in range(2):
                        x = g.xn[:, chunk(2 * b + u)]
                        for i in range(4):
                            if i == 0:
                                pe.wait_ge(xb_done, 4 * b)
                            if i == 2:
                                pe.wait_ge(z_done, 4 * b + 2 * u)
                            bank = 2 * u + i if i < 2 else 2 + i
                            pe.matmul(ps[:, bank, :], win[:, i, :], x, start=True, stop=True).then_inc(prod, 1)
                        if b0 is not None:
                            pe.wait_ge(b0_done, 2 * b)
                            pe.matmul(bps[:, u, :], wb0[:, :], x, start=True, stop=True).then_inc(b0_prod, 1)

            @block.vector
            def _(dve):
                dve.wait_ge(padded, 1)
                dve.wait_ge(loaded, 16 * len(loads))
                with dve.Fori(0, BATCH) as b:
                    for u in range(2):
                        for i in range(2):
                            dve.wait_ge(prod, 8 * b + 4 * u + i + 1)
                            dve.tensor_copy(xb[:, i, bass.ds(b, 1), 3 + u * CH:3 + (u + 1) * CH],
                                            ps[:, 2 * u + i, :].unsqueeze(1)).then_inc(xb_done, 1)
                        dve.wait_ge(silu_done, 4 * b + 2 * u)
                        for k in range(4):
                            for i in range(2):
                                src = xb[:, i, bass.ds(b, 1), u * CH + k:(u + 1) * CH + k].squeeze(1)
                                if k == 0:
                                    dve.wait_ge(xb_done, 4 * b + 2 * u + i + 1)
                                    dve.tensor_scalar(acc[:, i, 0, :], src, cw[:, i, 0:1], None, ALU.mult).then_inc(tap, 1)
                                else:
                                    dve.wait_ge(tap, 16 * b + 8 * u + 2 * (k - 1) + i + 1)
                                    dve.scalar_tensor_tensor(out=acc[:, i, k, :], in0=src, scalar=cw[:, i, k:k + 1],
                                                             in1=acc[:, i, k - 1, :], op0=ALU.mult,
                                                             op1=ALU.add).then_inc(tap, 1)

            @block.scalar
            def _(act):
                act.wait_ge(loaded, 16 * len(loads))
                with act.Fori(0, BATCH) as b:
                    for u in range(2):
                        for i in range(2):
                            act.wait_ge(prod, 8 * b + 4 * u + 3 + i)
                            act.wait_ge(z_stored[u], 16 * b)
                            act.activation(zt[:, u, i, :], ps[:, 4 + i, :], z_func).then_inc(z_done, 1)
                        if b0 is not None:
                            act.wait_ge(b0_prod, 2 * b + u + 1)
                            act.wait_ge(loaded, 16 * len(loads))
                            act.copy(b0[:, chunk(2 * b + u)], bps[:, u, :]).then_inc(b0_done, 1)
                        for i in range(2):
                            act.wait_ge(tap, 16 * b + 8 * u + 6 + i + 1)
                            act.wait_ge(loaded, 16 * len(loads))
                            act.activation(xs[:, i, chunk(2 * b + u)], acc[:, i, 3, :], ACT.Silu,
                                           bias=cb[:, i:i + 1]).then_inc(silu_done, 1)



def mamba_dt_stage(nc, g, name, w, xs, dt, bcs):
    with Stage(nc, name) as s:
        wx, wdt, bdt = s.sb("wx", [P, 2, 96]), s.sb("wdt", [64, 2, P]), s.sb("bdt", [P, 2])
        dtl = s.sb("dtl", [64, 2, CH])
        ab, ex, ln, lost, pos, sm = (s.sb(x, [P, 2, CH]) for x in ("ab", "ex", "ln", "lost", "pos", "sm"))
        rest, mid = s.sb("rest", [32, CH]), s.sb("mid", [32, CH], BF16)
        lp, bp, vp = s.ps("lp", [64, 2, CH]), s.ps("bp", [32, 2, CH]), s.ps("vp", [P, 2, CH])
        warm = s.sb("warm", [P, 1])
        (loaded, low_ready, bc_ready, low_copied, v_ready, exp_done, ln_done, lost_done, corr_done, sum_done, dt_done,
         bc_step, table, pos_done) = (s.sem(x) for x in (
             "loaded", "low_ready", "bc_ready", "low_copied", "v_ready", "exp_done", "ln_done", "lost_done",
             "corr_done", "sum_done", "dt_done", "bc_step", "table", "pos_done"))
        ab_done = s.sem("ab_done")
        with nc.Block() as block:
            @block.sync
            def _(sp):
                for d, n in ((wx, "wx"), (wdt, "wdt"), (bdt, "bdt")):
                    sp.dma_start(d[...], w[n]).then_inc(loaded, 16)

            @block.tensor
            def _(pe):
                pe.wait_ge(loaded, 48)
                with pe.Fori(0, NCH // 2) as m:
                    for u in range(2):
                        pe.wait_ge(low_copied, 2 * m)
                        pe.wait_ge(bc_step, 10 * m)
                        for i in range(2):
                            mm = pe.matmul(lp[:, u, :], wx[:, i, 0:64], xs[:, i, chunk(2 * m + u)], start=i == 0, stop=i == 1)
                        mm.then_inc(low_ready, 1)
                        for i in range(2):
                            mm = pe.matmul(bp[:, u, :], wx[:, i, 64:96], xs[:, i, chunk(2 * m + u)], start=i == 0, stop=i == 1)
                        mm.then_inc(bc_ready, 1)
                        pe.wait_ge(low_copied, 2 * m + u + 1)
                        for i in range(2):
                            pe.wait_ge(pos_done, 4 * m + 2 * u)
                            pe.wait_ge(ab_done, 4 * m + 2 * u)
                            pe.matmul(vp[:, i, :], wdt[:, i, :], dtl[:, u, :], start=True, stop=True).then_inc(v_ready, 1)

            @block.scalar
            def _(act):
                act.wait_ge(loaded, 48)
                act.activation(warm[:, :], g.eps[:, :], ACT.Ln).then_inc(table, 1)
                with act.Fori(0, NCH // 2) as m:
                    for u in range(2):
                        act.wait_ge(low_ready, 2 * m + u + 1)
                        act.copy(dtl[:, u, :], lp[:, u, :]).then_inc(low_copied, 1)
                        for i in range(2):
                            k = 4 * m + 2 * u + i
                            act.wait_ge(pos_done, k + 1)
                            act.activation(ab[:, i, :], vp[:, i, :], ACT.Abs, bias=bdt[:, i:i + 1]).then_inc(ab_done, 1)
                            act.wait_ge(ab_done, k + 1)
                            act.wait_ge(corr_done, 4 * m + 2 * u)
                            act.activation(ex[:, i, :], ab[:, i, :], ACT.Exp, scale=-1.0).then_inc(exp_done, 1)
                            act.wait_ge(exp_done, k + 1)
                            act.wait_ge(sum_done, 4 * m + 2 * u)
                            act.activation(ln[:, i, :], ex[:, i, :], ACT.Ln, bias=g.ones[:, 0:1]).then_inc(ln_done, 1)

            @block.gpsimd
            def _(pool):
                with pool.Fori(0, NCH // 2) as m:
                    for u in range(2):
                        for i in range(2):
                            k = 4 * m + 2 * u + i
                            pool.wait_ge(lost_done, k + 1)
                            pool.tensor_tensor(lost[:, i, :], ex[:, i, :], lost[:, i, :], ALU.subtract).then_inc(corr_done, 1)
                            pool.wait_ge(ln_done, k + 1)
                            pool.wait_ge(corr_done, k + 1)
                            pool.wait_ge(dt_done, 4 * m + 2 * u)
                            pool.tensor_tensor(sm[:, i, :], ln[:, i, :], lost[:, i, :], ALU.add).then_inc(sum_done, 1)

            @block.vector
            def _(dve):
                dve.wait_ge(loaded, 48)
                with dve.Fori(0, NCH // 2) as m:
                    for u in range(2):
                        c = 2 * m + u
                        for i in range(2):
                            k = 4 * m + 2 * u + i
                            dve.wait_ge(v_ready, k + 1)
                            dve.wait_ge(dt_done, 4 * m + 2 * u)
                            dve.tensor_scalar(pos[:, i, :], vp[:, i, :], bdt[:, i:i + 1], 0.0, ALU.add, ALU.max).then_inc(pos_done, 1)
                            dve.wait_ge(exp_done, k + 1)
                            dve.wait_ge(sum_done, 4 * m + 2 * u)
                            dve.tensor_scalar(lost[:, i, :], ex[:, i, :], 1.0, -1.0, ALU.add, ALU.add).then_inc(lost_done, 1)
                        dve.wait_ge(bc_ready, c + 1)
                        st = lambda i: dve.wait_ge(bc_step, 5 * c + i)
                        dve.tensor_copy(bcs[0:32, chunk(c)], bp[:, u, :]).then_inc(bc_step, 1)
                        st(1)
                        dve.tensor_tensor(rest[:, :], bp[:, u, :], bcs[0:32, chunk(c)], ALU.subtract).then_inc(bc_step, 1)
                        st(2)
                        dve.tensor_copy(mid[:, :], rest[:, :]).then_inc(bc_step, 1)
                        st(3)
                        dve.tensor_copy(bcs[32:64, chunk(c)], mid[:, :]).then_inc(bc_step, 1)
                        dve.tensor_tensor(bcs[64:96, chunk(c)], rest[:, :], mid[:, :], ALU.subtract).then_inc(bc_step, 1)
                        for i in range(2):
                            k = 4 * m + 2 * u + i
                            dve.wait_ge(pos_done, k + 1)
                            dve.wait_ge(sum_done, k + 1)
                            dve.tensor_tensor(dt[:, i, chunk(c)], pos[:, i, :], sm[:, i, :], ALU.add).then_inc(dt_done, 1)
                dve.wait_ge(dt_done, 2 * NCH)
                dve.wait_ge(bc_step, 5 * NCH)


def mamba_scan_stage(nc, g, name, w, xs, dt, bcs, z_dram):
    with Stage(nc, name) as s:
        NS = 16
        self_ = g.xn[0:96, :].rearrange("p (n q) -> p n q", q=P)
        sel = s.sb("sel", [96, 2 * NS, P], BF16)
        aneg, dcol, wout = s.sb("aneg", [P, 2, NS]), s.sb("dcol", [P, 2]), s.sb("wout", [P, 2, P])
        alog = s.sb("alog", [P, 2, NS])
        bc_sb = s.sb("bc_sb", [P, 2, 2, SEQ])
        da, dbx = s.sb("da", [P, 4, SEQ]), s.sb("dbx", [P, 3, SEQ])
        hs = s.sb("hs", [P, 3, SEQ])
        hc = g.xn[:, :].rearrange("p (k t) -> p k t", t=SEQ)
        dtx, zb = s.sb("dtx", [P, 2, SEQ]), s.sb("zb", [P, 2, SEQ])
        yg = xs
        bps, cps, yps = s.ps("bps", [P, 2, CH]), s.ps("cps", [P, 2, CH]), s.ps("yps", [P, 2, 2, CH])
        (loaded, sel_in, sel_ready, a_ready, b_ready, c_ready, b_copied, c_copied, da_done, dtx_done, dbx_done,
         scan_done, hc_done, acc_done, y_used, yg_ready, o_ready, added, z_in, a_exp) = (s.sem(x) for x in (
             "loaded", "sel_in", "sel_ready", "a_ready", "b_ready", "c_ready", "b_copied", "c_copied", "da_done",
             "dtx_done", "dbx_done", "scan_done", "hc_done", "acc_done", "y_used", "yg_ready", "o_ready", "added",
             "z_in", "a_exp"))
        zs = z_dram.rearrange("(x p) t -> p x t", p=P)
        steps = 2 * NS
        batch = lambda b: bass.ds(b * SEQ, SEQ)
        with nc.Block() as block:
            @block.sync
            def _(sp):
                sp.dma_start(self_, w["sel"]).then_inc(sel_in, 16)
                for d, n in ((alog, "alog"), (dcol, "d"), (wout, "wout")):
                    sp.dma_start(d[...], w[n]).then_inc(loaded, 16)
                with sp.Fori(0, BATCH) as b:
                    sp.wait_ge(yg_ready, 2 * b)
                    sp.dma_start(zb[:, :, :], zs[:, :, batch(b)]).then_inc(z_in, 16)

            @block.tensor
            def _(pe):
                pe.wait_ge(sel_ready, 1)
                pe.wait_ge(loaded, 48)
                with pe.Fori(0, BATCH) as b:
                    def accumulate(n):
                        for i in range(2):
                            pe.wait_ge(hc_done, steps * b + 2 * n + i + 1)
                            for f in range(2):
                                mm = pe.matmul(yps[:, i, f, :], g.ident[:, :], hc[:, (2 * n + i) % 4, f * CH:(f + 1) * CH],
                                               start=n == 0, stop=n == NS - 1)
                            mm.then_inc(acc_done, 1)

                    for n in range(NS):
                        for copied, ready, ps, row in ((b_copied, b_ready, bps, n), (c_copied, c_ready, cps, NS + n)):
                            pe.wait_ge(copied, NS * b + n)
                            for f in range(2):
                                mm = pe.matmul(ps[:, f, :], sel[:, row, :], bcs[:, chunk(2 * b + f)], start=True, stop=True)
                            mm.then_inc(ready, 1)
                        if n == 2:
                            pe.wait_ge(y_used, 2 * b)
                        if n >= 2:
                            accumulate(n - 2)
                    accumulate(NS - 2)
                    accumulate(NS - 1)
                pe.wait_ge(yg_ready, 2 * BATCH)
                pe.wait_ge(b_copied, NS * BATCH)
                for c in range(NCH):
                    if c >= 2:
                        pe.wait_ge(added, c - 1)
                    for i in range(2):
                        mm = pe.matmul(bps[:, c % 2, :], wout[:, i, :], yg[:, i, chunk(c)], start=i == 0, stop=i == 1)
                    mm.then_inc(o_ready, 1)

            @block.scalar
            def _(act):
                act.wait_ge(loaded, 48)
                act.activation(aneg[:, :, :], alog[:, :, :], ACT.Exp).then_inc(a_exp, 1)
                act.wait_ge(a_exp, 1)
                act.mul(aneg[:, :, :], aneg[:, :, :], -1.0).then_inc(a_ready, 1)
                act.wait_ge(a_ready, 1)
                with act.Fori(0, BATCH) as b:
                    for n in range(NS):
                        before = steps * b + max(2 * n - 2, 0)
                        act.wait_ge(b_ready, NS * b + n + 1)
                        act.wait_ge(dbx_done, before)
                        act.wait_ge(scan_done, before)
                        act.copy(bc_sb[:, 0, n % 2, :], bps[:, :, :].rearrange("p f t -> p (f t)")).then_inc(b_copied, 1)
                        act.wait_ge(c_ready, NS * b + n + 1)
                        act.wait_ge(hc_done, before)
                        act.copy(bc_sb[:, 1, n % 2, :], cps[:, :, :].rearrange("p f t -> p (f t)")).then_inc(c_copied, 1)
                        for i in range(2):
                            k = 2 * n + i
                            act.activation(da[:, k % 4, :], dt[:, i, batch(b)], ACT.Exp,
                                           scale=aneg[:, i, n:n + 1]).then_inc(da_done, 1)

            @block.vector
            def _(dve):
                dve.wait_ge(loaded, 48)
                with dve.Fori(0, BATCH) as b:
                    def input_of(k):
                        n, i = k // 2, k % 2
                        dve.wait_ge(b_copied, NS * b + n + 1)
                        dve.wait_ge(dtx_done, 2 * b + i + 1)
                        dve.wait_ge(scan_done, steps * b + max(k - 2, 0))
                        dve.tensor_tensor(dbx[:, k % 3, :], dtx[:, i, :], bc_sb[:, 0, n % 2, :], ALU.mult).then_inc(dbx_done, 1)

                    for i in range(2):
                        dve.tensor_tensor(dtx[:, i, :], dt[:, i, batch(b)], xs[:, i, batch(b)], ALU.mult).then_inc(dtx_done, 1)
                    input_of(0)
                    for k in range(steps):
                        if k + 1 < steps:
                            input_of(k + 1)
                        dve.wait_ge(da_done, steps * b + k + 1)
                        dve.wait_ge(dbx_done, steps * b + k + 1)
                        dve.wait_ge(hc_done, steps * b + max(k - 2, 0))
                        dve.tensor_tensor_scan(hs[:, k % 3, :], da[:, k % 4, :], dbx[:, k % 3, :], 0.0,
                                               ALU.mult, ALU.add).then_inc(scan_done, 1)
                    dve.wait_ge(acc_done, steps * (b + 1))
                    for i in range(2):
                        dve.scalar_tensor_tensor(out=yg[:, i, batch(b)], in0=xs[:, i, batch(b)], scalar=dcol[:, i:i + 1],
                                                 in1=yps[:, i, :, :].rearrange("p f t -> p (f t)"), op0=ALU.mult,
                                                 op1=ALU.add).then_inc(y_used, 1)
                    dve.wait_ge(z_in, 16 * (b + 1))
                    for i in range(2):
                        dve.wait_ge(y_used, 2 * b + i + 1)
                        dve.tensor_tensor(yg[:, i, batch(b)], yg[:, i, batch(b)], zb[:, i, :], ALU.mult).then_inc(yg_ready, 1)
                for c in range(NCH):
                    dve.wait_ge(o_ready, c + 1)
                    x = g.xT[:, chunk(c)]
                    dve.tensor_tensor(x, x, bps[:, c % 2, :], ALU.add).then_inc(added, 1)
                dve.wait_ge(added, NCH)

            @block.gpsimd
            def _(pool):
                pool.wait_ge(sel_in, 16)
                pool.tensor_copy(sel[:, :, :], self_).then_inc(sel_ready, 1)
                pool.wait_ge(sel_ready, 1)
                with pool.Fori(0, BATCH) as b:
                    for k in range(steps):
                        n, i = k // 2, k % 2
                        pool.wait_ge(scan_done, steps * b + k + 1)
                        pool.wait_ge(c_copied, NS * b + n + 1)
                        pool.wait_ge(acc_done, steps * b + max(k - 3, 0))
                        pool.tensor_tensor(hc[:, k % 4, :], hs[:, k % 3, :], bc_sb[:, 1, n % 2, :], ALU.mult).then_inc(hc_done, 1)


def ssm_in_stage(nc, g, name, w, xs, b0, a_seq, bd, cc):
    with Stage(nc, name) as s:
        wx, wdt, row0 = s.sb("wx", [P, 2, 192]), s.sb("wdt", [64, P]), s.sb("row0", [P, P])
        bdt, aneg = s.sb("bdt", [P, 1]), s.sb("aneg", [P, 1])
        dr = s.sb("dr", [64, 2, CH])
        v, ab, ex, ln, lost, sp_ = (s.sb(x, [P, 2, CH]) for x in ("v", "ab", "ex", "ln", "lost", "sp"))
        dps, cps, vps, xps = s.ps("dps", [64, 2, CH]), s.ps("cps", [P, 2, CH]), s.ps("vps", [P, 2, CH]), s.ps("xps", [P, 2, CH])
        (loaded, dr_ready, c_ready, v_ready, x_ready, dr_copied, c_copied, v_done, ab_done, exp_done, ln_done, lost_done,
         step, bd_done, a_done, a_set, clipped, v_mul, capped) = (s.sem(x) for x in (
             "loaded", "dr_ready", "c_ready", "v_ready", "x_ready", "dr_copied", "c_copied", "v_done", "ab_done",
             "exp_done", "ln_done", "lost_done", "step", "bd_done", "a_done", "a_set", "clipped", "v_mul", "capped"))
        loads = ((wx, "wx"), (wdt, "wdt"), (row0, "row0"), (bdt, "bdt"), (aneg, "alog"))
        with nc.Block() as block:
            @block.sync
            def _(sp):
                for d, n in loads:
                    sp.dma_start(d[...], w[n]).then_inc(loaded, 16)

            @block.tensor
            def _(pe):
                pe.wait_ge(loaded, 16 * len(loads))
                with pe.Fori(0, NCH // 2) as m:
                    for u in range(2):
                        c = 2 * m + u
                        pe.wait_ge(dr_copied, 2 * m)
                        pe.wait_ge(c_copied, 2 * m)
                        pe.wait_ge(bd_done, 2 * m)
                        for i in range(2):
                            mm = pe.matmul(dps[:, u, :], wx[:, i, 0:64], xs[:, i, chunk(c)], start=i == 0, stop=i == 1)
                        mm.then_inc(dr_ready, 1)
                        for i in range(2):
                            mm = pe.matmul(cps[:, u, :], wx[:, i, 64:192], xs[:, i, chunk(c)], start=i == 0, stop=i == 1)
                        mm.then_inc(c_ready, 1)
                        pe.matmul(xps[:, u, :], row0[:, :], xs[:, 0, chunk(c)], start=True, stop=True).then_inc(x_ready, 1)
                        pe.wait_ge(dr_copied, c + 1)
                        pe.matmul(vps[:, u, :], wdt[:, :], dr[:, u, :], start=True, stop=True).then_inc(v_ready, 1)

            @block.scalar
            def _(act):
                act.wait_ge(loaded, 16 * len(loads))
                act.activation(ab[:, 0, 0:1], g.ones[:, 0:1], ACT.Ln).then_inc(a_set, 1)
                act.wait_ge(capped, 1)
                act.activation(aneg[:, :], aneg[:, :], ACT.Exp).then_inc(a_set, 1)
                act.wait_ge(a_set, 2)
                act.mul(aneg[:, :], aneg[:, :], -1.0).then_inc(a_set, 1)
                act.wait_ge(a_set, 3)
                with act.Fori(0, NCH // 2) as m:
                    for u in range(2):
                        c = 2 * m + u
                        act.wait_ge(dr_ready, c + 1)
                        act.copy(dr[:, u, :], dps[:, u, :]).then_inc(dr_copied, 1)
                        act.wait_ge(c_ready, c + 1)
                        act.wait_ge(a_set, 3)
                        act.copy(cc[:, chunk(c)], cps[:, u, :]).then_inc(c_copied, 1)
                        for i in range(2):
                            k = 2 * c + i
                            act.wait_ge(v_done, k + 1)
                            act.activation(ab[:, i, :], v[:, i, :], ACT.Abs).then_inc(ab_done, 1)
                            act.wait_ge(ab_done, k + 1)
                            act.activation(ex[:, i, :], ab[:, i, :], ACT.Exp, scale=-1.0).then_inc(exp_done, 1)
                            act.wait_ge(exp_done, k + 1)
                            act.activation(ln[:, i, :], ex[:, i, :], ACT.Ln, bias=g.ones[:, 0:1]).then_inc(ln_done, 1)
                        act.wait_ge(clipped, c + 1)
                        act.wait_ge(a_set, 3)
                        act.activation(a_seq[:, chunk(c)], sp_[:, 0, :], ACT.Exp, scale=aneg[:, :]).then_inc(a_done, 1)

            @block.vector
            def _(dve):
                dve.wait_ge(loaded, 16 * len(loads))
                dve.tensor_scalar(aneg[:, :], aneg[:, :], 30.0, None, ALU.min).then_inc(capped, 1)
                with dve.Fori(0, NCH // 2) as m:
                    for u in range(2):
                        c = 2 * m + u
                        dve.wait_ge(a_done, c)
                        dve.wait_ge(bd_done, c)
                        dve.wait_ge(v_ready, c + 1)
                        dve.tensor_scalar(v[:, 0, :], vps[:, u, :], bdt[:, :], None, ALU.add).then_inc(v_done, 1)
                        dve.tensor_copy(v[:, 1, :], b0[:, chunk(c)]).then_inc(v_done, 1)
                        for i in range(2):
                            k = 2 * c + i
                            dve.wait_ge(exp_done, k + 1)
                            dve.tensor_scalar(lost[:, i, :], ex[:, i, :], 1.0, -1.0, ALU.add, ALU.add).then_inc(lost_done, 1)
                            dve.wait_ge(lost_done, k + 1)
                            dve.tensor_tensor(lost[:, i, :], ex[:, i, :], lost[:, i, :], ALU.subtract).then_inc(step, 1)
                            dve.wait_ge(ln_done, k + 1)
                            dve.wait_ge(step, 3 * k + 1)
                            dve.tensor_tensor(lost[:, i, :], ln[:, i, :], lost[:, i, :], ALU.add).then_inc(step, 1)
                            dve.wait_ge(step, 3 * k + 2)
                            dve.scalar_tensor_tensor(out=sp_[:, i, :], in0=v[:, i, :], scalar=0.0, in1=lost[:, i, :],
                                                     op0=ALU.max, op1=ALU.add).then_inc(step, 1)
                            if i == 0:
                                dve.wait_ge(step, 3 * k + 3)
                                dve.tensor_scalar(sp_[:, 0, :], sp_[:, 0, :], 1e-6, 100.0, ALU.max, ALU.min).then_inc(clipped, 1)
                        dve.wait_ge(step, 6 * c + 6)
                        dve.wait_ge(clipped, c + 1)
                        dve.tensor_tensor(v[:, 1, :], sp_[:, 0, :], sp_[:, 1, :], ALU.mult).then_inc(v_mul, 1)
                        dve.wait_ge(v_mul, c + 1)
                        dve.wait_ge(x_ready, c + 1)
                        dve.tensor_tensor(bd[:, chunk(c)], v[:, 1, :], xps[:, u, :], ALU.mult).then_inc(bd_done, 1)
                dve.wait_ge(bd_done, NCH)


def ssm_scan_stage(nc, g, name, w, xs, a_seq, bd, cc):
    with Stage(nc, name) as s:
        hs, cs, dcol = s.sb("hs", [P, 2, SEQ]), s.sb("cs", [P, 2, SEQ]), s.sb("dcol", [P, 2])
        ps = s.ps("ps", [P, 4, 2, CH])
        loaded, scanned, weighed, summed, done = (s.sem(x) for x in ("loaded", "scanned", "weighed", "summed", "done"))
        with nc.Block() as block:
            @block.sync
            def _(sp):
                sp.dma_start(dcol[:, :], w["d"]).then_inc(loaded, 16)

            @block.vector
            def _(dve):
                def scan(b):
                    w_ = slice(b * SEQ, (b + 1) * SEQ)
                    dve.tensor_tensor_scan(hs[:, b % 2, :], a_seq[:, w_], bd[:, w_], 0.0, ALU.mult, ALU.add).then_inc(scanned, 1)
                    dve.wait_ge(scanned, b + 1)
                    if b >= 2:
                        dve.wait_ge(summed, b - 1)
                    dve.tensor_tensor(cs[:, b % 2, :], hs[:, b % 2, :], cc[:, w_], ALU.mult).then_inc(weighed, 1)

                dve.wait_ge(loaded, 16)
                scan(0)
                for b in range(BATCH):
                    if b + 1 < BATCH:
                        scan(b + 1)
                    dve.wait_ge(summed, b + 1)
                    for i in range(2):
                        x = xs[:, i, b * SEQ:(b + 1) * SEQ]
                        dve.scalar_tensor_tensor(out=x, in0=x, scalar=dcol[:, i:i + 1],
                                                 in1=ps[:, b, :, :].rearrange("p f t -> p (f t)"), op0=ALU.mult,
                                                 op1=ALU.add).then_inc(done, 1)
                dve.wait_ge(done, 2 * BATCH)

            @block.tensor
            def _(pe):
                for b in range(BATCH):
                    pe.wait_ge(weighed, b + 1)
                    for f in range(2):
                        mm = pe.matmul(ps[:, b, f, :], g.ones[:, :], cs[:, b % 2, f * CH:(f + 1) * CH], start=True, stop=True)
                    mm.then_inc(summed, 1)


def ssm_out_stage(nc, g, name, w, yn, z_dram):
    with Stage(nc, name) as s:
        wout = s.sb("wout", [P, 2, P])
        lg, lb, rs = s.sb("lg", [P, 2]), s.sb("lb", [P, 2]), s.sb("rs", [P, 1])
        zt, sg, yg = s.sb("zt", [P, 2, 2, CH]), s.sb("sg", [P, 2, 2, CH]), s.sb("yg", [P, 2, 2, CH])
        ps = s.ps("ps", [P, 2, CH])
        loaded, z_in, sig_done = s.sem("loaded"), [s.sem(f"z_in{u}") for u in range(2)], s.sem("sig_done")
        affine, gated, o_ready, added = (s.sem(x) for x in ("affine", "gated", "o_ready", "added"))
        loads = ((wout, "wout"), (lg, "lg"), (lb, "lb"), (rs, "rs"))
        zs = z_dram.rearrange("(x p) t -> p x t", p=P)
        with nc.Block() as block:
            @block.sync
            def _(sp):
                for d, n in loads:
                    sp.dma_start(d[...], w[n]).then_inc(loaded, 16)
                with sp.Fori(0, NCH // 2) as m:
                    for u in range(2):
                        sp.wait_ge(sig_done, 2 * m)
                        sp.dma_start(zt[:, u, :, :], zs[:, :, chunk(2 * m + u)]).then_inc(z_in[u], 16)

            @block.scalar
            def _(act):
                with act.Fori(0, NCH // 2) as m:
                    for u in range(2):
                        act.wait_ge(z_in[u], 16 * (m + 1))
                        act.wait_ge(gated, 4 * m)
                        act.activation(sg[:, u, :, :], zt[:, u, :, :], ACT.Sigmoid).then_inc(sig_done, 1)

            @block.vector
            def _(dve):
                dve.wait_ge(loaded, 16 * len(loads))
                with dve.Fori(0, NCH // 2) as m:
                    for u in range(2):
                        c = 2 * m + u
                        for i in range(2):
                            y = yn[:, i, chunk(c)]
                            dve.tensor_scalar(y, y, lg[:, i:i + 1], lb[:, i:i + 1], ALU.mult, ALU.add).then_inc(affine, 1)
                        dve.wait_ge(sig_done, c + 1)
                        dve.wait_ge(o_ready, 2 * m)
                        for i in range(2):
                            dve.wait_ge(affine, 2 * c + i + 1)
                            dve.tensor_tensor(yg[:, u, i, :], yn[:, i, chunk(c)], sg[:, u, i, :], ALU.mult).then_inc(gated, 1)
                        dve.wait_ge(o_ready, c + 1)
                        x = g.xT[:, chunk(c)]
                        dve.scalar_tensor_tensor(out=x, in0=ps[:, u, :], scalar=rs[:, :], in1=x, op0=ALU.mult,
                                                 op1=ALU.add).then_inc(added, 1)
                dve.wait_ge(added, NCH)

            @block.tensor
            def _(pe):
                pe.wait_ge(loaded, 16 * len(loads))
                with pe.Fori(0, NCH // 2) as m:
                    for u in range(2):
                        pe.wait_ge(added, 2 * m)
                        for i in range(2):
                            pe.wait_ge(gated, 4 * m + 2 * u + i + 1)
                            mm = pe.matmul(ps[:, u, :], wout[:, i, :], yg[:, u, i, :], start=i == 0, stop=i == 1)
                        mm.then_inc(o_ready, 1)


def spike_stage(nc, g, name, w):
    tiles, steps = 4, 5
    with Stage(nc, name) as s:
        wfc, wproj = s.sb("wfc", [P, tiles, P]), s.sb("wproj", [P, tiles, P])
        r, h = s.sb("r", [P, 2, CH]), s.sb("h", [P, 3, CH])
        y, u_, mem, cnt = (s.sb(x, [P, 2, CH]) for x in ("y", "u", "mem", "cnt"))
        zp, yp = s.ps("zp", [P, 3, CH]), s.ps("yp", [P, 2, CH])
        loaded, z_ready, relu_done, h_done = (s.sem(x) for x in ("loaded", "z_ready", "relu_done", "h_done"))
        y_ready, y_copied, step, added = (s.sem(x) for x in ("y_ready", "y_copied", "step", "added"))
        per = 1 + 3 * (steps - 1)
        with nc.Block() as block:
            @block.sync
            def _(sp):
                sp.dma_start(wfc[...], w["wfc"]).then_inc(loaded, 16)
                sp.dma_start(wproj[...], w["wproj"]).then_inc(loaded, 16)

            @block.tensor
            def _(pe):
                pe.wait_ge(loaded, 32)
                with pe.Fori(0, NCH // 2) as m:
                    def down(j):
                        u, t = j // tiles, j % tiles
                        if t == 0:
                            pe.wait_ge(y_copied, 2 * m)
                        pe.wait_ge(h_done, 8 * m + j + 1)
                        mm = pe.matmul(yp[:, u, :], wproj[:, t, :], h[:, j % 3, :], start=t == 0, stop=t == tiles - 1)
                        if t == tiles - 1:
                            mm.then_inc(y_ready, 1)

                    for j in range(2 * tiles):
                        u, t = j // tiles, j % tiles
                        pe.matmul(zp[:, j % 2, :], wfc[:, t, :], g.xn[:, chunk(2 * m + u)],
                                  start=True, stop=True).then_inc(z_ready, 1)
                        if j >= 1:
                            down(j - 1)
                    down(2 * tiles - 1)

            @block.scalar
            def _(act):
                with act.Fori(0, NCH // 2) as m:
                    for j in range(2 * tiles):
                        act.wait_ge(z_ready, 8 * m + j + 1)
                        act.activation(r[:, j % 2, :], zp[:, j % 2, :], ACT.Relu).then_inc(relu_done, 1)
                        act.wait_ge(relu_done, 8 * m + j + 1)
                        act.activation(h[:, j % 3, :], r[:, j % 2, :], ACT.Square).then_inc(h_done, 1)
                        if j % tiles == tiles - 1:
                            u = j // tiles
                            act.wait_ge(added, 2 * m)
                            act.wait_ge(y_ready, 2 * m + u + 1)
                            act.copy(y[:, u, :], yp[:, u, :]).then_inc(y_copied, 1)

            @block.vector
            def _(dve):
                with dve.Fori(0, NCH // 2) as m:
                    for u in range(2):
                        c = 2 * m + u
                        k = [0]

                        def link(ins):
                            k[0] += 1
                            ins.then_inc(step, 1)
                            dve.wait_ge(step, per * c + k[0])

                        dve.wait_ge(y_copied, c + 1)
                        link(dve.tensor_scalar(cnt[:, u, :], y[:, u, :], 1.0, None, ALU.is_gt))
                        last = y
                        for t in range(1, steps):
                            link(dve.scalar_tensor_tensor(out=u_[:, u, :], in0=last[:, u, :], scalar=0.9,
                                                          in1=y[:, u, :], op0=ALU.mult, op1=ALU.add))
                            link(dve.scalar_tensor_tensor(out=mem[:, u, :], in0=last[:, u, :], scalar=1.0,
                                                          in1=u_[:, u, :], op0=ALU.is_gt, op1=ALU.subtract, reverse1=True))
                            link(dve.scalar_tensor_tensor(out=cnt[:, u, :], in0=mem[:, u, :], scalar=1.0,
                                                          in1=cnt[:, u, :], op0=ALU.is_gt, op1=ALU.add))
                            last = mem
                        x = g.xT[:, chunk(c)]
                        dve.scalar_tensor_tensor(out=x, in0=cnt[:, u, :], scalar=1.0 / steps, in1=x, op0=ALU.mult,
                                                 op1=ALU.add).then_inc(added, 1)
                dve.wait_ge(added, NCH)


def build(nc, a, out, stop=99, start=0):
    layer = lambda p: {n[len(p):]: a[n] for n in a if n.startswith(p)}
    with ExitStack() as ctx:
        g = Globals()
        g.ctx = ctx
        buffer = lambda n, shape, dt=F32: ctx.enter_context(nc.sbuf_tensor("g_" + n, shape, dt))
        g.xT, g.xn = buffer("xT", [P, TOK]), buffer("xn", [P, TOK])
        g.ident, g.ident_b = buffer("ident", [P, P]), buffer("ident_b", [P, P], BF16)
        g.ones, g.eps = buffer("ones", [P, P]), buffer("eps", [P, 1])
        load_stage(nc, g, a["x"], a["ident"])
        if start <= 0 < stop:
            norm_stage(nc, g, "n0")
            attention(nc, g, "a0", layer("a0_"), True, HD ** -0.5, a["a0_bo"], None)
        if start <= 1 < stop:
            norm_stage(nc, g, "n1")
            w = layer("f0_")
            with nc.sbuf_tensor("f0_comb", [27, TOK], BF16) as combT:
                top2_stage(nc, g, "f0r", w["gate"], w["desc"], combT, 8, False)
                glu_stage(nc, g, "f0", 14, w, combT, 27)
        if start <= 2 < stop:
            norm_stage(nc, g, "n2")
            attention(nc, g, "a1", layer("a1_"), False, HD ** -0.5 / P, None,
                      SEQ / float(np.sqrt(SEQ - 1.0)) * SEQ ** -0.5 / P)
        if start <= 3 < stop:
            norm_stage(nc, g, "n3")
            w = layer("f1_")
            with nc.sbuf_tensor("f1_mask", [8, TOK], F32) as maskT, nc.sbuf_tensor("f1_maskb", [8, TOK], BF16) as maskb:
                top1_stage(nc, g, "f1r", w, maskT, maskb)
                expert_stage(nc, g, "f1", w, maskT, maskb)
        if start <= 4 < stop:
            norm_stage(nc, g, "n4")
            w = layer("m2_")
            z_dram = nc.dram_tensor("m2_z", [2 * P, TOK], F32, kind="Internal").ap()
            with nc.sbuf_tensor("m2_xs", [P, 2, TOK], F32) as xs:
                conv_in_stage(nc, g, "m2i", w, xs, z_dram, ACT.Silu, None)
                with nc.sbuf_tensor("m2_dt", [P, 2, TOK], F32) as dt, nc.sbuf_tensor("m2_bcs", [96, TOK], BF16) as bcs:
                    mamba_dt_stage(nc, g, "m2d", w, xs, dt, bcs)
                    mamba_scan_stage(nc, g, "m2s", w, xs, dt, bcs, z_dram)
        if start <= 5 < stop:
            norm_stage(nc, g, "n5")
            w = layer("f2_")
            with nc.sbuf_tensor("f2_comb", [51, TOK], BF16) as combT:
                top2_stage(nc, g, "f2r", w["gate"], w["desc"], combT, 16, True)
                glu_stage(nc, g, "f2", 9, w, combT, 51)
        if start <= 6 < stop:
            norm_stage(nc, g, "n6")
            w = layer("m3_")
            z_dram = nc.dram_tensor("m3_z", [2 * P, TOK], F32, kind="Internal").ap()
            with nc.sbuf_tensor("m3_xs", [P, 2, TOK], F32) as xs:
                with nc.sbuf_tensor("m3_b0", [P, TOK], F32) as b0:
                    conv_in_stage(nc, g, "m3i", w, xs, z_dram, ACT.Copy, b0)
                    with nc.sbuf_tensor("m3_a", [P, TOK], F32) as a_seq, nc.sbuf_tensor("m3_bd", [P, TOK], F32) as bd, \
                            nc.sbuf_tensor("m3_c", [P, TOK], F32) as cc:
                        ssm_in_stage(nc, g, "m3p", w, xs, b0, a_seq, bd, cc)
                        ssm_scan_stage(nc, g, "m3s", w, xs, a_seq, bd, cc)
                tiles = [xs[:, 0, :], xs[:, 1, :]]
                norm_stage(nc, g, "m3n", tiles, tiles)
                ssm_out_stage(nc, g, "m3o", w, xs, z_dram)
        if start <= 7 < stop:
            norm_stage(nc, g, "n7")
            spike_stage(nc, g, "f3", layer("f3_"))
        store_stage(nc, g, out)


def _layout(i):
    f = np.float32
    c = np.ascontiguousarray
    i = {n: np.asarray(v) for n, v in i.items()}
    col = lambda v: c(v.reshape(-1, 1))
    rep = lambda v: c(np.broadcast_to(v.reshape(1, -1), (P, v.size)))
    a = {"x": i["L0_attn_hidden_states"], "ident": np.eye(P, dtype=f)}
    dm = np.arange(P).reshape(HEADS, HD).T.reshape(-1)
    swap = np.arange(P).reshape(HEADS, HD).copy()
    swap[:, :6] = swap[:, [1, 0, 3, 2, 5, 4]]
    swap = swap.reshape(-1)[dm]
    ids = np.arange(SEQ)
    pos = (ids // 256, (ids % 256) // 16, ids % 16)
    cos, sin = np.ones((HD, SEQ), f), np.zeros((HD, SEQ), f)
    for d in range(6):
        cos[d] = np.cos(pos[d // 2].astype(f))
        sin[d] = np.sin(pos[d // 2].astype(f)) * (1 if d % 2 else -1)
    a["a0_cos"], a["a0_sin"] = np.repeat(cos, HEADS, 0), np.repeat(sin, HEADS, 0)
    p = "L0_attn_"
    for n in "qk":
        a[f"a0_w{n}"], a[f"a0_w{n}r"] = c(i[p + "W" + n][:, dm]), c(i[p + "W" + n][:, swap])
        a[f"a0_b{n}"], a[f"a0_b{n}r"] = col(i[p + "b" + n][dm]), col(i[p + "b" + n][swap])
    a["a0_wv"], a["a0_bv"], a["a0_wo"], a["a0_bo"] = i[p + "Wv"], rep(i[p + "bv"]), i[p + "Wo"], col(i[p + "bo"])

    def glu(pre, gate, up, down, split, experts, size):
        n = gate.shape[0]
        tiles = -(-n // P)
        pad = lambda w: np.concatenate([w, np.zeros((tiles * P - n, P), f)])
        a[pre + "wg"] = c(pad(gate).reshape(tiles, P, P).transpose(2, 0, 1))
        a[pre + "wu"] = c(pad(up).reshape(tiles, P, P).transpose(2, 0, 1))
        a[pre + "wd"] = c(pad(down).reshape(tiles, P, P).transpose(1, 0, 2))
        row = np.minimum(np.arange(tiles * P) // size, experts)
        sel = (row[None, :] == np.arange(experts + 1)[:, None]).astype(f)
        a[pre + "sel"] = np.concatenate([sel] * 3).reshape(-1, tiles, P)
        a[pre + "gate"] = c(split.T)
        a[pre + "desc"] = rep(np.arange(experts, 0, -1).astype(f))

    p, half = "L0_ffn_", 192
    up = i[p + "w_up"]
    glu("f0_", np.concatenate([up[:, :half].reshape(-1, P), i[p + "sg_gate"]]),
        np.concatenate([up[:, half:].reshape(-1, P), i[p + "sg_up"]]),
        np.concatenate([i[p + "w_down"].transpose(0, 2, 1).reshape(-1, P), i[p + "sg_down"].T]),
        i[p + "gate_w"], 8, half)
    p = "L1_attn_"
    w = i[p + "w_qkv"].T
    a["a1_wq"], a["a1_wk"], a["a1_wv"] = c(w[:, dm]), c(w[:, P + dm]), c(w[:, 2 * P:])
    a["a1_wo"] = c(i[p + "w_o"].T)
    p = "L1_ffn_"
    e, ff = 8, 512
    a["f1_gate"], a["f1_desc"] = c(i[p + "router_w"].T), rep(np.arange(e, 0, -1).astype(f))
    a["f1_before"] = np.triu(np.ones((P, P), f), 1)
    a["f1_sel"] = c(np.broadcast_to(np.eye(e, dtype=f)[:, :, None], (e, e, P)))
    a["f1_w1"] = c(i[p + "W1"].reshape(e, P, 4, P).transpose(1, 0, 2, 3).reshape(P, 4 * e, P))
    a["f1_w2"] = c(i[p + "W2"].reshape(4 * e, P, P).transpose(1, 0, 2))
    a["f1_b1"], a["f1_b2"] = c(i[p + "b1"].reshape(4 * e, P).T), i[p + "b2"]
    p = "L2_ffn_"
    w1, ws1 = i[p + "W1"], i[p + "Ws1"]
    glu("f2_", np.concatenate([w1[:, :, 64:].transpose(0, 2, 1).reshape(-1, P), ws1[:, P:].T]),
        np.concatenate([w1[:, :, :64].transpose(0, 2, 1).reshape(-1, P), ws1[:, :P].T]),
        np.concatenate([i[p + "W2"].reshape(-1, P), i[p + "Ws2"]]), i[p + "Wg"], 16, 64)
    p = "L2_attn_"
    tile2 = lambda v: c(v.reshape(2, P, -1).transpose(1, 0, 2))
    col2 = lambda v: c(v.reshape(2, P).T)
    a["m2_win"] = c(i[p + "W_in"].reshape(P, 4, P))
    a["m2_cw"], a["m2_cb"] = tile2(i[p + "conv_w"]), col2(i[p + "conv_b"])
    a["m2_wx"], a["m2_wdt"], a["m2_bdt"] = tile2(i[p + "W_x"]), c(i[p + "W_dt"].reshape(64, 2, P)), col2(i[p + "b_dt"])
    a["m2_alog"], a["m2_d"], a["m2_wout"] = tile2(i[p + "A_log"]), col2(i[p + "D"]), tile2(i[p + "W_out"])
    a["m2_sel"] = np.concatenate([np.broadcast_to(np.eye(32, dtype=f)[:, :, None], (32, 32, P))] * 3)
    p = "L3_attn_"
    a["m3_win"] = c(i[p + "Win"][:, :4 * P].reshape(P, 4, P))
    a["m3_wb0"] = c(np.broadcast_to(i[p + "Win"][:, 4 * P:4 * P + 1], (P, P)))
    a["m3_cw"], a["m3_cb"] = tile2(i[p + "conv_w"]), col2(i[p + "conv_b"])
    a["m3_wx"], a["m3_wdt"] = tile2(i[p + "Wx"]), c(np.broadcast_to(i[p + "Wdt"][:, 0:1], (64, P)))
    a["m3_row0"] = np.repeat((np.arange(P) == 0).astype(f)[:, None], P, 1)
    a["m3_bdt"] = c(np.broadcast_to(i[p + "bdt"][0:1].reshape(1, 1), (P, 1)))
    a["m3_alog"] = col(i[p + "A_log"][0])
    a["m3_d"], a["m3_lg"], a["m3_lb"] = col2(i[p + "D"]), col2(i[p + "ln_g"]), col2(i[p + "ln_b"])
    a["m3_wout"] = tile2(i[p + "Wout"])
    a["m3_rs"] = c(np.broadcast_to(i[p + "res_scale"].reshape(1, 1), (P, 1)))
    p = "L3_ffn_"
    a["f3_wfc"] = c(i[p + "W_fc"].reshape(4, P, P).transpose(2, 0, 1))
    a["f3_wproj"] = c(i[p + "W_proj"].T.reshape(4, P, P).transpose(1, 0, 2))
    return a


def kernel(**inputs):
    import concourse.bacc as _bacc
    from concourse.bass_utils import run_bass_kernel_spmd as _run

    nc = _bacc.Bacc("TRN2", target_bir_lowering=False, num_devices=1)
    arrays, aps = {}, {}
    for name, v in _layout(inputs).items():
        v = np.ascontiguousarray(v)
        arrays[f"in_{name}_dram"] = v
        aps[name] = nc.dram_tensor(f"in_{name}_dram", v.shape, mybir.dt.from_np(v.dtype), kind="ExternalInput").ap()
    out = nc.dram_tensor("out_0_dram", (BATCH, SEQ, P), F32, kind="ExternalOutput").ap()
    build(nc, aps, out)
    r = _run(nc, [arrays], core_ids=[0])
    return r.results[0]["out_0_dram"]
```
